# Optimizing a Trainium2 kernel written in Bass

```python
import numpy as np
import jax
import jax.numpy as jnp

def _softmax(x, axis=-1):
    return jax.nn.softmax(x, axis=axis)

def _gelu(x):
    return jax.nn.gelu(x, approximate=True)

def _silu(x):
    return jax.nn.silu(x)

def _sigmoid(x):
    return jax.nn.sigmoid(x)

def _layernorm(x, axis=-1, eps=1e-05):
    m = jnp.mean(x, axis=axis, keepdims=True)
    v = jnp.var(x, axis=axis, keepdims=True)
    return (x - m) / jnp.sqrt(v + eps)

def _scatter_add(tgt, idx, src, axis=0):
    return tgt.at[idx].add(src)

def _segment_sum(src, seg, n):
    return jax.ops.segment_sum(src, seg, n)
kernel_name = 'mk_prb_d1_jaxref_r8_047af4'

def setup_inputs(seed: int=0):
    np.random.seed(seed)
    _w = jnp.asarray

    def _L0_attn_setup():
        import math
        import jax, jax.numpy as jnp
        import numpy as np
        D_MODEL = 128
        N_HEADS = 16
        HEAD_DIM = D_MODEL // N_HEADS

        def build_rope_cache(seq_len, head_dim):
            half = head_dim // 2
            inv_freq = 1.0 / 10000.0 ** (jnp.arange(half, dtype=jnp.float32) / half)
            pos = jnp.arange(seq_len, dtype=jnp.float32)
            angles = jnp.outer(pos, inv_freq)
            return (jnp.cos(angles)[None, None], jnp.sin(angles)[None, None])

        def apply_rope(x, cos, sin):
            half = x.shape[-1] // 2
            x1, x2 = (x[..., :half], x[..., half:])
            return jnp.concatenate((x1 * cos - x2 * sin, x1 * sin + x2 * cos), axis=-1)
        key = jax.random.key(seed)
        ks = jax.random.split(key, 5)
        B, S = (2, 256)
        bound = 1.0 / math.sqrt(D_MODEL)
        x = jax.random.normal(ks[0], (B, S, D_MODEL), dtype=jnp.float32)
        qkv_w = jax.random.uniform(ks[1], (3 * D_MODEL, D_MODEL), minval=-bound, maxval=bound, dtype=jnp.float32)
        qkv_b = jax.random.uniform(ks[2], (3 * D_MODEL,), minval=-bound, maxval=bound, dtype=jnp.float32)
        out_w = jax.random.uniform(ks[3], (D_MODEL, D_MODEL), minval=-bound, maxval=bound, dtype=jnp.float32)
        out_b = jax.random.uniform(ks[4], (D_MODEL,), minval=-bound, maxval=bound, dtype=jnp.float32)
        return {'x': x, 'qkv_w': qkv_w, 'qkv_b': qkv_b, 'out_w': out_w, 'out_b': out_b}
    _L0_attn_in = _L0_attn_setup()

    def _L0_ffn_setup():
        import jax, jax.numpy as jnp
        import numpy as np
        NUM_NOD = 6
        MAX_PREV = 5
        NUM_EDGE = 20
        D = 128
        H = 8
        LN_EPS = 1e-06

        def _layernorm(x, g, b):
            mu = jnp.mean(x, axis=-1, keepdims=True)
            var = jnp.mean(jnp.square(x - mu), axis=-1, keepdims=True)
            return (x - mu) * jax.lax.rsqrt(var + LN_EPS) * g + b

        def _mha(q, k, v, wq, wk, wv, wo):
            B, S, d = q.shape
            dh = d // H
            qh = (q @ wq).reshape(B, S, H, dh)
            kh = (k @ wk).reshape(B, S, H, dh)
            vh = (v @ wv).reshape(B, S, H, dh)
            scores = jnp.einsum('bqhd,bkhd->bhqk', qh, kh) / jnp.sqrt(jnp.asarray(dh, q.dtype))
            attn = jax.nn.softmax(scores, axis=-1)
            ctx = jnp.einsum('bhqk,bkhd->bqhd', attn, vh).reshape(B, S, d)
            return ctx @ wo
        key = jax.random.key(seed)
        ks = jax.random.split(key, 12)
        B, S = (8, 128)
        scale = 1.0 / np.sqrt(D)
        return {'inputs': jax.random.normal(ks[0], (B, S, D), jnp.float32), 'ew': jax.random.uniform(ks[1], (NUM_NOD, 3), jnp.float32), 'act_w': jax.random.uniform(ks[2], (NUM_NOD,), jnp.float32), 'We': jax.random.normal(ks[3], (NUM_EDGE, D, D), jnp.float32) * scale, 'be': jnp.zeros((NUM_EDGE, D), jnp.float32), 'Wq': jax.random.normal(ks[4], (NUM_NOD, D, D), jnp.float32) * scale, 'Wk': jax.random.normal(ks[5], (NUM_NOD, D, D), jnp.float32) * scale, 'Wv': jax.random.normal(ks[6], (NUM_NOD, D, D), jnp.float32) * scale, 'Wo': jax.random.normal(ks[7], (NUM_NOD, D, D), jnp.float32) * scale, 'ln_g': jnp.ones((D,), jnp.float32), 'ln_b': jnp.zeros((D,), jnp.float32)}
    _L0_ffn_in = _L0_ffn_setup()
    _d = {'L0_attn_x': _L0_attn_in['x'], 'L0_attn_qkv_w': _L0_attn_in['qkv_w'], 'L0_attn_qkv_b': _L0_attn_in['qkv_b'], 'L0_attn_out_w': _L0_attn_in['out_w'], 'L0_attn_out_b': _L0_attn_in['out_b'], 'L0_ffn_ew': _L0_ffn_in['ew'], 'L0_ffn_act_w': _L0_ffn_in['act_w'], 'L0_ffn_We': _L0_ffn_in['We'], 'L0_ffn_be': _L0_ffn_in['be'], 'L0_ffn_Wq': _L0_ffn_in['Wq'], 'L0_ffn_Wk': _L0_ffn_in['Wk'], 'L0_ffn_Wv': _L0_ffn_in['Wv'], 'L0_ffn_Wo': _L0_ffn_in['Wo'], 'L0_ffn_ln_g': _L0_ffn_in['ln_g'], 'L0_ffn_ln_b': _L0_ffn_in['ln_b']}
    _x0 = _d['L0_attn_x']
    _d['L0_attn_x'] = jax.random.normal(jax.random.fold_in(jax.random.key(seed), 1), (2, 1024, 128), dtype=_x0.dtype)
    del _x0
    return _d

def reference(L0_attn_x, L0_attn_qkv_w, L0_attn_qkv_b, L0_attn_out_w, L0_attn_out_b, L0_ffn_ew, L0_ffn_act_w, L0_ffn_We, L0_ffn_be, L0_ffn_Wq, L0_ffn_Wk, L0_ffn_Wv, L0_ffn_Wo, L0_ffn_ln_g, L0_ffn_ln_b):

    def _L0_attn_ref(x, qkv_w, qkv_b, out_w, out_b):
        import math
        import jax, jax.numpy as jnp
        import numpy as np
        D_MODEL = 128
        N_HEADS = 16
        HEAD_DIM = D_MODEL // N_HEADS

        def build_rope_cache(seq_len, head_dim):
            half = head_dim // 2
            inv_freq = 1.0 / 10000.0 ** (jnp.arange(half, dtype=jnp.float32) / half)
            pos = jnp.arange(seq_len, dtype=jnp.float32)
            angles = jnp.outer(pos, inv_freq)
            return (jnp.cos(angles)[None, None], jnp.sin(angles)[None, None])

        def apply_rope(x, cos, sin):
            half = x.shape[-1] // 2
            x1, x2 = (x[..., :half], x[..., half:])
            return jnp.concatenate((x1 * cos - x2 * sin, x1 * sin + x2 * cos), axis=-1)
        B, S, D = x.shape
        H, Hd = (N_HEADS, HEAD_DIM)
        qkv = x @ qkv_w.T + qkv_b
        qkv = qkv.reshape(B, S, 3, H, Hd).transpose(2, 0, 3, 1, 4)
        q, k, v = (qkv[0], qkv[1], qkv[2])
        cos, sin = build_rope_cache(S, Hd)
        q = apply_rope(q, cos, sin)
        k = apply_rope(k, cos, sin)
        scores = jnp.einsum('bhqd,bhkd->bhqk', q, k) / math.sqrt(Hd)
        causal = jnp.triu(jnp.ones((S, S), dtype=bool), k=1)
        scores = jnp.where(causal, jnp.finfo(scores.dtype).min, scores)
        attn = jax.nn.softmax(scores, axis=-1)
        out = jnp.einsum('bhqk,bhkd->bhqd', attn, v)
        out = out.transpose(0, 2, 1, 3).reshape(B, S, D)
        return out @ out_w.T + out_b

    def _L0_ffn_ref(inputs, ew, act_w, We, be, Wq, Wk, Wv, Wo, ln_g, ln_b):
        import jax, jax.numpy as jnp
        import numpy as np
        NUM_NOD = 6
        MAX_PREV = 5
        NUM_EDGE = 20
        D = 128
        H = 8
        LN_EPS = 1e-06

        def _layernorm(x, g, b):
            mu = jnp.mean(x, axis=-1, keepdims=True)
            var = jnp.mean(jnp.square(x - mu), axis=-1, keepdims=True)
            return (x - mu) * jax.lax.rsqrt(var + LN_EPS) * g + b

        def _mha(q, k, v, wq, wk, wv, wo):
            B, S, d = q.shape
            dh = d // H
            qh = (q @ wq).reshape(B, S, H, dh)
            kh = (k @ wk).reshape(B, S, H, dh)
            vh = (v @ wv).reshape(B, S, H, dh)
            scores = jnp.einsum('bqhd,bkhd->bhqk', qh, kh) / jnp.sqrt(jnp.asarray(dh, q.dtype))
            attn = jax.nn.softmax(scores, axis=-1)
            ctx = jnp.einsum('bhqk,bkhd->bqhd', attn, vh).reshape(B, S, d)
            return ctx @ wo
        nodes = {-1: inputs}
        lind = 0
        for c in range(NUM_NOD):
            nsrc = min(c + 1, MAX_PREV)
            snode = c - nsrc
            eq, ek, ev = (lind + nsrc - 1, lind, lind + nsrc // 2)
            in_q, in_k, in_v = (c - 1, snode, snode + nsrc // 2)
            q = ew[c, 0] * (nodes[in_q] @ We[eq] + be[eq])
            k = ew[c, 1] * (nodes[in_k] @ We[ek] + be[ek])
            v = ew[c, 2] * (nodes[in_v] @ We[ev] + be[ev])
            o = _mha(q, k, v, Wq[c], Wk[c], Wv[c], Wo[c])
            nodes[c] = act_w[c] * o + q
            lind += nsrc
        out = nodes[NUM_NOD - 1]
        return _layernorm(out, ln_g, ln_b)
    x = L0_attn_x
    xn = _layernorm(x, axis=-1)
    x = x + _L0_attn_ref(xn, L0_attn_qkv_w, L0_attn_qkv_b, L0_attn_out_w, L0_attn_out_b) + _L0_ffn_ref(xn, L0_ffn_ew, L0_ffn_act_w, L0_ffn_We, L0_ffn_be, L0_ffn_Wq, L0_ffn_Wk, L0_ffn_Wv, L0_ffn_Wo, L0_ffn_ln_g, L0_ffn_ln_b)
    return x

_drawn_inputs = setup_inputs


def setup_inputs(seed=0):
    import zlib

    import numpy as np

    out = dict(_drawn_inputs(seed))
    spreads = {'L0_ffn_be': (0.0, 0.1), 'L0_ffn_ln_g': (1.0, 0.2), 'L0_ffn_ln_b': (0.0, 0.1)}
    factors = {'L0_ffn_Wq': 64.0, 'L0_ffn_Wk': 64.0}
    for name, (base, spread) in spreads.items():
        noise = np.random.default_rng([zlib.crc32(name.encode()), seed]).standard_normal(out[name].shape)
        drawn = base * np.exp(spread * noise) if base else spread * noise
        out[name] = jnp.asarray(drawn.astype(out[name].dtype))
    for name, factor in factors.items():
        out[name] = (out[name] * factor).astype(out[name].dtype)
    return out
```

```python
import concourse.bass as bass
from concourse import mybir
from contextlib import ExitStack

F32 = mybir.dt.float32
BF16 = mybir.dt.bfloat16
ACT = mybir.ActivationFunctionType
ALU = mybir.AluOpType
AX = mybir.AxisListType

D = 128
NB, S = 2, 1024
T = NB * S
TT = T // 128
TB = S // 128
CH = 512
NCH = S // CH
HA, DA = 16, 8
HB, DB = 8, 16
NODES, PREV = 6, 5
UP = 8
RING = 4
STAGES = 4
KROW = 96
MROW = KROW
KALL = KROW + 3
GQ = 256
VW = 32
LROW = 16
SCALE_A, SCALE_B = DA ** -0.5, DB ** -0.5
EPS_A, EPS_B = 1e-5, 1e-6
MASKED = -1e30
Q_ROWS = [(0, 3, 1), (3, 6, 2), (4, 5, 1)]
K_ROWS = [(2, 5, 1), (1, 6, 4), (0, 1, 1)]


def edges():
    first, out = 0, []
    for c in range(NODES):
        n = min(c + 1, PREV)
        out.append(((first + n - 1, first, first + n // 2), (c, c - n + 1, c - n + 1 + n // 2)))
        first += n
    return out


def pieces(kind, j):
    w = S - 128 * j if kind == "A" else S
    return [(lo, min(lo + CH, w)) for lo in range(0, w, CH)]


N_PIECES = {k: sum(len(pieces(k, j)) for j in range(TB)) for k in "AB"}
KINDS = ["A0", "AL", "B0", "BL", "BE", "T"]
TIMES = {"A0": 1, "AL": 3, "B0": 1, "BL": 10, "BE": 1, "T": 1}
MT_SLOT = 3
PREP_AT = {(5, 0): ("q", 0), (5, 2): ("q", 1), (5, 4): ("k", 0), (5, 6): ("k", 1),
           (6, 0): ("v", 0), (6, 4): ("v", 1)}
NODE_AT = {(4, 2): ("node", 0), (4, 5): ("node", 1)}
XA_AT = {(6, 2): ("xa", 0), (6, 6): ("xa", 1), (7, 0): ("xa", 2), (7, 2): ("xa", 3)}
FIN_AT = {(4, 2): ("fin", 0), (4, 5): ("fin", 1)}

KINDS = ["A0", "AL", "AZ", "B0", "BL", "BE", "T"]
TIMES = {"A0": 1, "AL": NB * HA // UP - 2, "AZ": 1, "B0": 1, "BL": (NODES - 1) * NB, "BE": 1, "T": 1}
EXTRA = {"A0": PREP_AT, "AL": {}, "AZ": {}, "B0": {**PREP_AT, **XA_AT}, "BL": {**NODE_AT, **PREP_AT},
         "BE": FIN_AT, "T": {}}
PREPARES = ("A0", "B0", "BL")
STEPS = {k: 3 if k == "T" else UP for k in KINDS}


def kind_at(kind, k, lag):
    if k - lag >= 0:
        return None if kind == "T" else kind[0]
    return {"A0": None, "AL": "A", "AZ": "A", "B0": "A", "BL": "B", "BE": "B", "T": "B"}[kind]


class Count:

    def __init__(self, **per):
        self.per = {k: per.get(k, 0) for k in KINDS}

    def before(self, kind, r):
        n = sum(self.per[x] * TIMES[x] for x in KINDS[:KINDS.index(kind)])
        return n + r * self.per[kind] if TIMES[kind] > 1 and self.per[kind] else n

    def after(self, kind, r):
        return self.before(kind, r) + self.per[kind]


def pieces_before(kind, k):
    return sum(N_PIECES[kind_at(kind, u, 2)] for u in range(k) if kind_at(kind, u, 2))


PHASES = Count(A0=1, AL=1, AZ=1, B0=1, BL=1, BE=1)
PIECES = Count(**{k: pieces_before(k, STEPS[k]) for k in KINDS})
PREPS = Count(A0=1, B0=1, BL=1)
PREP_STEPS = Count(**{k: len(EXTRA[k]) for k in ("A0", "BL")}, B0=len(PREP_AT))
NODE_PHASES = Count(BL=1)
NORMS = Count(B0=NB, BL=1, BE=1, T=1)
CUR_COPIES = Count(BL=4)
CUR_FIRST = 2
N_CONST = 10 + 5 * RING


def piece_no(kind, k, j):
    which = kind_at(kind, k, 2)
    return pieces_before(kind, k) + sum(len(pieces(which, t)) for t in range(j))


def prep_no(kind, what, w):
    steps = [v for _, v in sorted(EXTRA[kind].items()) if v[0] != "xa"]
    return steps.index((what, w)) + 1


def dual_attention_kernel(nc, x, w_qk, w_va, w_oa, b_a, out_b, cos, sin, ew, act_w, we_t, we_q,
                          be, wq, wk, wv, wo, ln_g, ln_b, out):
    ctx = ExitStack()
    with ctx:
        def sb(name, shape, dt=F32):
            return ctx.enter_context(nc.sbuf_tensor(name, shape, dt))

        def pb(name, shape, dt=F32):
            return ctx.enter_context(nc.psum_tensor(name, shape, dt))

        def sem(name):
            return ctx.enter_context(nc.semaphore(name))

        qk_dram = {"A": nc.dram_tensor("dram_qk_a", (2, 6, NB * HA * DA, S), BF16).ap(),
                   "B": nc.dram_tensor("dram_qk_b", (2, 6, NB * HB * DB, S), BF16).ap()}
        raw_dram = {"A": nc.dram_tensor("dram_raw_a", (NB * HA, 128, GQ), F32).ap(),
                    "B": nc.dram_tensor("dram_raw_b", (NB * HB, 128, GQ), F32).ap()}
        rec_dram = {"A": nc.dram_tensor("dram_rec_a", (NB, HA, S), F32).ap(),
                    "B": nc.dram_tensor("dram_rec_b", (NB, HB, S), F32).ap()}

        srcT = sb("srcT", [128, NODES * T])
        xtok = sb("xtok", [128, TT * D])
        qs = [sb(f"qs{s}", [128, S], BF16) for s in range(RING)]
        ks = [sb(f"ks{s}", [128, S], BF16) for s in range(RING)]
        vs = [sb(f"vs{s}", [128, TB, VW]) for s in range(RING)]
        probs = [sb(f"probs{s}", [128, S]) for s in range(RING)]
        vtok_a = sb("vtok_a", [128, TT * D])
        vtok_b = sb("vtok_b", [128, NB * TB * D])
        comp = sb("comp", [128, NODES * 5 * D])
        cur = sb("cur", [128, 4 * D])
        cur_bias = sb("cur_bias", [128, 3])
        bias_b = sb("bias_b", [128, NODES * 3])
        w_a = sb("w_a", [128, 6 * D])
        bias_a = sb("bias_a", [128, 5])
        ctx_a = sb("ctx_a", [128, T])
        table = sb("table", [128, 2 * S])
        ctx_b = sb("ctx_b", [128, S])
        rec_b = sb("rec_b", [128, S])
        vsrc = sb("vsrc", [128, S])
        full = [sb(f"full{s}", [128, CH]) for s in range(STAGES)]
        parts = [sb(f"parts{s}", [128, 3, CH], BF16) for s in range(STAGES)]
        csb = [sb(f"csb{s}", [128, GQ]) for s in range(2)]
        neg_max = [sb(f"neg_max{s}", [128, TB]) for s in range(2)]
        mres = sb("mres", [128, TB])
        mparts = [sb(f"mparts{s}", [128, 3 * TB], BF16) for s in range(2)]
        mrows = [sb(f"mrows{s}", [3 * TB, 128], BF16) for s in range(2)]
        sums = sb("sums", [128, 4 * 64])
        rope = [sb(f"rope{s}", [128, CH]) for s in range(2)]
        ident = sb("ident", [128, 128])
        ident_h = sb("ident_h", [128, 128], BF16)
        mask_q = sb("mask_q", [128, 128], BF16)
        mask_k = sb("mask_k", [128, 128], BF16)
        ones_row = sb("ones_row", [1, 128])
        ewb = sb("ewb", [128, NODES * 3])
        actb = sb("actb", [128, NODES])
        be_sb = sb("be_sb", [128, NODES * 3])
        vbias = sb("vbias", [128, NODES * 3])
        row_o = sb("row_o", [1, 128])
        row_n = sb("row_n", [1, 128])
        lng = sb("lng", [128, D])
        lnb = sb("lnb", [128, D])
        stats = sb("stats", [128, TT * 6])
        mv = sb("mv", [128, TT * 2])
        rstd = sb("rstd", [128, TT])
        power = sb("power", [128, TT])
        zeros = sb("zeros", [128, CH])
        fin = sb("fin", [128, T])

        raw_w = srcT[:, 2 * T:5 * T]
        we_t_sb = raw_w[:, 0:NODES * 3 * D]
        we_q_sb = raw_w[:, NODES * 3 * D:NODES * 4 * D]
        w4_sb = raw_w[:, NODES * 4 * D:NODES * 8 * D]
        xn = fin

        s1 = [pb(f"s1_{n}", [128, S]) for n in range(2)]
        s2 = [pb(f"s2_{n}", [128, CH]) for n in range(2)]
        cps = pb("cps", [128, CH])
        misc = pb("misc", [128, CH])

        sems = ("x_in wa_in wb_in pool_const ln_stats ln_pow xn_ready xt_ps xt_sb dve_order rot_ps rot_done "
                "rope_full rope_hi rope_res rope_mid a_low va_ps va_sb comp_ps comp_sb wo_ready bias_ps vbias_ready "
                "node_bias_ps bias_done row_ps row_sb spread_ps pro_done cur_ready s1_ready max_done max_parts "
                "mt_ready mrow_sb s2_ready exp_done pv_done ctx_sb vs_ready prep_ps prep_full parts_done v_ready "
                "node_ready vsrc_in sums_in ctx_in rec_ready rec_out rec_in ctx_ready xa_ps xa_done fin_ps fin_sb "
                "fin_stats fin_pow out_ready stored")
        (x_in, wa_in, wb_in, pool_const, ln_stats, ln_pow, xn_ready, xt_ps, xt_sb, dve_order, rot_ps, rot_done,
         rope_full, rope_hi, rope_res, rope_mid, a_low, va_ps, va_sb, comp_ps, comp_sb, wo_ready, bias_ps,
         vbias_ready, node_bias_ps, bias_done, row_ps, row_sb, spread_ps, pro_done, cur_ready, s1_ready, max_done,
         max_parts, mt_ready, mrow_sb, s2_ready, exp_done, pv_done, ctx_sb, vs_ready, prep_ps, prep_full,
         parts_done, v_ready, node_ready, vsrc_in, sums_in, ctx_in, rec_ready, rec_out, rec_in, ctx_ready, xa_ps,
         xa_done, fin_ps, fin_sb, fin_stats, fin_pow, out_ready, stored) = [sem(n) for n in sems.split()]
        qk_in = [sem(f"qk_in{n}") for n in range(RING)]
        mrow_in = [sem(f"mrow_in{n}") for n in range(RING)]
        ctx_out = [sem(f"ctx_out{n}") for n in range(2)]
        written = sem("written")
        a_written = [sem(f"a_written{n}") for n in range(STAGES)]
        half = [s1[n // 2][:, n % 2 * CH:(n % 2 + 1) * CH] for n in range(4)]
        misc_rows = misc[0:3 * TB, 0:64].bitcast(BF16)

        def need(eng, s, value):
            if isinstance(value, int) and value <= 0:
                return
            eng.wait_ge(s, value)

        def walk(eng, phase):
            phase("A0", 0, 0, 0)
            with eng.Fori(0, TIMES["AL"]) as r:
                phase("AL", r, 0, 0)
            phase("AZ", 0, 0, 0)
            phase("B0", 0, 0, 1)
            with eng.Fori(1, NODES) as c:
                with eng.Fori(0, NB) as b:
                    phase("BL", (c - 1) * NB + b, c, b)
            phase("BE", 0, 0, 0)
            phase("T", 0, 0, 1)

        def head_row(kind, r, k, b):
            if kind[0] == "A" or kind == "B0" and k < 0:
                return {"A0": 0, "AL": r * UP + UP, "AZ": 3 * UP, "B0": 4 * UP}[kind] + k
            here = {"B0": 0, "BL": b * -1 + 1, "BE": 1, "T": 0}[kind]
            other = {"B0": 1, "BL": b, "BE": 0, "T": 1}[kind]
            return here * HB + k if 0 <= k < UP else other * HB + k % UP

        block = ctx.enter_context(nc.Block())

        @block.sync
        def _(sp):
            xt = x.rearrange("(t p) d -> p t d", p=128)
            for h in range(NB):
                sp.dma_start(xtok[:, h * S:(h + 1) * S].rearrange("p (t d) -> p t d", d=D),
                             xt[:, h * TB:(h + 1) * TB, :]).then_inc(x_in, 16)
            sp.dma_start(w_a[:, 0:4 * D], w_qk).then_inc(wa_in, 16)
            sp.dma_start(w_a[:, 4 * D:5 * D], w_va).then_inc(wa_in, 16)
            sp.dma_start(w_a[:, 5 * D:6 * D], w_oa).then_inc(wa_in, 16)
            sp.dma_start(bias_a[:, :], b_a).then_inc(wa_in, 16)
            sp.dma_start(table[:, 0:S], cos).then_inc(wa_in, 16)
            sp.dma_start(table[:, S:2 * S], sin).then_inc(wa_in, 16)
            sp.dma_start(row_o[:, :], out_b).then_inc(wa_in, 16)
            sp.dma_start(ewb[:, :], ew.partition_broadcast(128)).then_inc(wb_in, 16)
            sp.dma_start(actb[:, :], act_w.partition_broadcast(128)).then_inc(wb_in, 16)
            sp.dma_start(be_sb[:, :], be).then_inc(wb_in, 16)
            sp.dma_start(we_t_sb, we_t).then_inc(wb_in, 16)
            sp.dma_start(we_q_sb.rearrange("p (n d) -> p n d", n=NODES),
                         we_q.rearrange("n p d -> p n d")).then_inc(wb_in, 16)
            for n, w in enumerate((wq, wk, wv, wo)):
                sp.dma_start(w4_sb[:, n * NODES * D:(n + 1) * NODES * D].rearrange("p (n d) -> p n d", n=NODES),
                             w.rearrange("n p d -> p n d")).then_inc(wb_in, 16)
            sp.dma_start(lng[:, :], ln_g.partition_broadcast(128)).then_inc(wb_in, 16)
            sp.dma_start(lnb[:, :], ln_b.partition_broadcast(128)).then_inc(wb_in, 16)

            def write_parts(which, n, rows, op, w, done):
                for part, (lo, hi, step) in enumerate((Q_ROWS, K_ROWS)[op]):
                    groups = len(range(lo, hi, step))
                    sp.dma_start(qk_dram[which][op, lo:hi:step, rows, w * CH:(w + 1) * CH
                                                ].rearrange("r p s -> p r s"),
                                 parts[n % STAGES][:, part:part + 1, :].broadcast_to([128, groups, CH])
                                 ).then_inc(done, 16)

            n = 0
            for b in range(NB):
                for w in range(NCH):
                    for op in range(2):
                        sp.wait_ge(a_low, n + 1)
                        write_parts("A", n, slice(b * 128, (b + 1) * 128), op, w, a_written[n % STAGES])
                        n += 1
            for s in a_written:
                sp.wait_ge(s, 3 * 16 * n // STAGES)

            def load_unit(kind, r, k, b):
                which = "B" if kind[0] == "B" or (kind, k) == ("AZ", UP) else "A"
                row = 0 if (kind, k) == ("AZ", UP) else head_row(kind, r, k, b)
                width, slot = (DA, DB)[which == "B"], k % RING
                if k < UP:
                    need(sp, pv_done, TB * (UP * PHASES.before(kind, r) + k - RING + 1))
                else:
                    sp.wait_ge(written, 4 * 3 * 16 * PREPS.after(kind, r))
                for op, dst in ((0, qs[slot]), (1, ks[slot])):
                    sp.dma_start(dst[0:6 * width, :],
                                 qk_dram[which][op, :, bass.ds(row * width, width), :]
                                 ).then_inc(qk_in[slot], 16)

            sp.wait_ge(pool_const, N_CONST)
            load_unit("A0", 0, 0, 0)

            def norm_batches(kind, b):
                return {"B0": [0, 1], "BL": [b], "BE": [0], "T": [1]}.get(kind, [])

            def read_contexts(kind, r, b):
                which, heads, width = ("A", HA, DA) if kind == "B0" else ("B", HB, DB)
                cols = heads * S // 128
                for n, batch in enumerate(norm_batches(kind, b)):
                    raw = raw_dram[which][bass.ds(batch * heads, heads), :, :]
                    sp.dma_start(sums[:, n * cols:(n + 1) * cols],
                                 raw[:, LROW:128:VW, :].rearrange("h g (a n) -> h g a n", n=cols)
                                 ).then_inc(sums_in, 16)
                    dst = ctx_a[:, n * S:(n + 1) * S] if which == "A" else ctx_b
                    for g in range(S // GQ):
                        sp.dma_start(dst[:, g * GQ:(g + 1) * GQ], raw[:, g * VW:g * VW + width, :]
                                     ).then_inc(ctx_in, 16)

            def spread_reciprocals(kind, r, b):
                which, heads, width = ("A", HA, DA) if kind == "B0" else ("B", HB, DB)
                cols = heads * S // 128
                sp.wait_ge(rec_ready, NORMS.after(kind, r))
                for n, batch in enumerate(norm_batches(kind, b)):
                    sp.dma_start(rec_dram[which][bass.ds(batch, 1), :, :].rearrange("o h (a n) -> (o h a) n", n=cols),
                                 sums[:, n * cols:(n + 1) * cols]).then_inc(rec_out, 16)
                sp.wait_ge(rec_out, 16 * NORMS.after(kind, r))
                for n, batch in enumerate(norm_batches(kind, b)):
                    dst = table[:, n * S:(n + 1) * S] if which == "A" else rec_b[:, :]
                    src = rec_dram[which][bass.ds(batch, 1), :, :].rearrange("o h n -> (o h) n")
                    sp.dma_start(dst, src.unsqueeze(1).broadcast_to([heads, width, S])).then_inc(rec_in, 16)

            def phase(kind, r, c, b):
                ph = PHASES.before(kind, r)
                for k in range(STEPS[kind]):
                    u = UP * ph + k
                    if k < UP - 1 and kind != "T":
                        load_unit(kind, r, k + 1, b)
                    if kind_at(kind, k, 3):
                        sp.wait_ge(ctx_sb, u - 2)
                        sp.dma_start(raw_dram[kind_at(kind, k, 3)][bass.ds(head_row(kind, r, k - 3, b), 1), :, :
                                                                   ].rearrange("o p n -> (o p) n"),
                                     csb[(k - 3) % 2][:, :]).then_inc(ctx_out[(k - 3) % 2], 16)
                    if NORMS.per[kind] and k == 2:
                        for s in ctx_out:
                            sp.wait_ge(s, 16 * (UP // 2) * ph)
                        sp.wait_ge(prep_ps, PREP_STEPS.before(kind, r))
                        if kind == "T":
                            sp.wait_ge(fin_ps, 2)
                        read_contexts(kind, r, b)
                    if NORMS.per[kind] and k == (2 if kind == "T" else 3):
                        spread_reciprocals(kind, r, b)
                    if kind_at(kind, k, 1):
                        sp.wait_ge(mrow_sb, u)
                        sp.dma_start(qs[(k - 1) % RING][MROW:KALL, :].rearrange("a (i n) -> a i n", n=128),
                                     mrows[(k - 1) % 2][:, :]).then_inc(mrow_in[(k - 1) % RING], 16)
                    if kind in PREPARES and k == 5:
                        need(sp, node_ready, 2 * NODE_PHASES.after(kind, r))
                        need(sp, prep_ps, PREP_STEPS.before(kind, r))
                        sp.dma_start(vsrc[:, :], srcT[:, bass.ds((c + 1) // 2 * T + b * S, S)]
                                     ).then_inc(vsrc_in, 16)
                    if kind in PREPARES and k in (5, 6):
                        for n in {5: (0, 1), 6: (2, 3)}[k]:
                            sp.wait_ge(parts_done, 3 * (4 * PREPS.before(kind, r) + n + 1))
                            write_parts("B", n, bass.ds(b * 128, 128), n // 2, n % 2, written)
                    if k == UP - 1 and kind not in ("BE", "T"):
                        load_unit(kind, r, UP, b)

            walk(sp, phase)
            for b in range(NB):
                sp.wait_ge(out_ready, b + 1)
                sp.dma_start(out.rearrange("(t p) d -> p t d", p=128)[:, b * TB:(b + 1) * TB, :],
                             fin[:, b * S:(b + 1) * S].rearrange("p (t d) -> p t d", d=D)).then_inc(stored, 16)
            sp.wait_ge(stored, 16 * NB)
            for s in ctx_out:
                sp.wait_ge(s, 16 * UP // 2 * (NB * HA // UP + NODES * NB))
            sp.wait_ge(written, 4 * 3 * 16 * NODES * NB)
            sp.wait_ge(rec_out, 16 * NORMS.after("T", 0))

        @block.gpsimd
        def _(pool):
            pl = nc.gpsimd
            pl.memset(ident[:, :], 0.0).then_inc(pool_const, 1)
            pl.memset(mask_q[:, :], 0.0).then_inc(pool_const, 1)
            pl.memset(mask_k[:, :], 0.0).then_inc(pool_const, 1)
            pool.wait_ge(pool_const, 3)
            pl.affine_select(out=ident[:, :], in_=ident[:, :], pattern=[[-1, 128]], compare_op=ALU.not_equal,
                             fill=1.0, base=0, channel_multiplier=1).then_inc(pool_const, 1)
            pl.memset(power[:, :], -0.5).then_inc(pool_const, 1)
            pool.wait_ge(pool_const, 5)
            pl.tensor_copy(ident_h[:, :], ident[:, :]).then_inc(pool_const, 1)
            pool.wait_ge(ln_stats, 1)
            pl.tensor_tensor(rstd[:, :], rstd[:, :], power[:, :], ALU.pow).then_inc(ln_pow, 1)
            pl.affine_select(out=mask_q[:, :], in_=mask_q[:, :], pattern=[[-1, 128]], compare_op=ALU.is_ge,
                             fill=MASKED, base=0, channel_multiplier=1).then_inc(pool_const, 1)
            pl.affine_select(out=mask_k[:, :], in_=mask_k[:, :], pattern=[[1, 128]], compare_op=ALU.is_ge,
                             fill=MASKED, base=0, channel_multiplier=-1).then_inc(pool_const, 1)
            pl.memset(ones_row[:, :], 1.0).then_inc(pool_const, 1)
            pl.memset(zeros[:, :], 0.0).then_inc(pool_const, 1)
            for s in range(RING):
                pl.memset(qs[s][:, :], 0.0).then_inc(pool_const, 1)
                pl.memset(ks[s][:, :], 0.0).then_inc(pool_const, 1)
                pl.memset(vs[s][:, :, :], 0.0).then_inc(pool_const, 1)
            pool.wait_ge(pool_const, N_CONST - 2 * RING)
            for s in range(RING):
                pl.memset(vs[s][:, :, LROW:LROW + 1], 1.0).then_inc(pool_const, 1)
            for s in range(RING):
                pool.wait_ge(pool_const, N_CONST - RING + s)
                pl.memset(ks[s][MROW:128, :], 1.0).then_inc(pool_const, 1)
            pool.wait_ge(pool_const, N_CONST)
            for n in range(2 * NB * NCH):
                pool.wait_ge(rope_mid, n + 1)
                pl.tensor_tensor(parts[n % STAGES][:, 2, :], full[n % STAGES][:, :], parts[n % STAGES][:, 1, :],
                                 ALU.subtract).then_inc(a_low, 1)
            pool.wait_ge(comp_sb, 3 * NODES)
            pool.wait_ge(bias_done, 1)
            pl.tensor_copy(cur[:, 0:2 * D], comp[:, 0:2 * D]).then_inc(cur_ready, 1)
            pl.tensor_copy(cur_bias[:, 0:2], bias_b[:, 0:2]).then_inc(cur_ready, 1)

            def phase(kind, r, c, b):
                ph = PHASES.before(kind, r)
                for k in range(STEPS[kind]):
                    u = UP * ph + k
                    if kind_at(kind, k, 1):
                        v, nm, mp = u - 1, neg_max[(k - 1) % 2], mparts[(k - 1) % 2]
                        pool.wait_ge(max_done, TB * u)
                        need(pool, mt_ready, v - 1)
                        pl.tensor_tensor(mp[:, 0:TB], nm[:, :], zeros[:, 0:TB], ALU.add).then_inc(max_parts, 1)
                        pool.wait_ge(max_parts, 4 * v + 1)
                        pl.tensor_tensor(mres[:, :], nm[:, :], mp[:, 0:TB], ALU.subtract).then_inc(max_parts, 1)
                        pool.wait_ge(max_parts, 4 * v + 2)
                        pl.tensor_tensor(mp[:, TB:2 * TB], mres[:, :], zeros[:, 0:TB], ALU.add).then_inc(max_parts, 1)
                        pool.wait_ge(max_parts, 4 * v + 3)
                        pl.tensor_tensor(mp[:, 2 * TB:3 * TB], mres[:, :], mp[:, TB:2 * TB],
                                         ALU.subtract).then_inc(max_parts, 1)
                    if kind != "T":
                        which = kind[0]
                        width = (DA, DB)[which == "B"]
                        batch = {"A0": 0, "AL": r, "AZ": 1, "B0": 0, "BL": b * -1 + 1, "BE": 1}[kind]
                        head = {"AL": (r * -1 + 1) * UP, "AZ": UP}.get(kind, 0) + k
                        need(pool, pv_done, TB * (u - RING + 1))
                        if kind == "A0" and k == 0:
                            pool.wait_ge(va_sb, TT // 4)
                        if which == "B":
                            pool.wait_ge(v_ready, NCH * PREPS.before(kind, r) if kind != "B0" else NCH)
                        src = (vtok_a, vtok_b)[which == "B"][:, :].rearrange("p (t d) -> p t d", d=D)
                        pl.tensor_copy(vs[k % RING][:, :, 0:width],
                                       src[:, bass.ds(batch * TB, TB), bass.ds(head * width, width)]
                                       ).then_inc(vs_ready, 1)
                    if kind == "BL" and k == 0:
                        pool.wait_ge(mrow_sb, u - 1)
                        pl.tensor_tensor(cur[:, 0:2 * D], comp[:, bass.ds(c * 5 * D, 2 * D)], zeros[:, 0:2 * D],
                                         ALU.add).then_inc(cur_ready, 1)
                        pl.tensor_copy(cur[:, 2 * D:4 * D], comp[:, bass.ds(c * 5 * D - 2 * D, 2 * D)]
                                       ).then_inc(cur_ready, 1)
                        pl.tensor_copy(cur_bias[:, 0:2], bias_b[:, bass.ds(c * 3, 2)]).then_inc(cur_ready, 1)
                        pl.tensor_copy(cur_bias[:, 2:3], bias_b[:, bass.ds(c * 3 - 1, 1)]).then_inc(cur_ready, 1)
                    if NORMS.per[kind] and k == (2 if kind == "T" else 3):
                        pool.wait_ge(rec_in, 16 * NORMS.after(kind, r))
                        pool.wait_ge(ctx_in, 16 * (S // GQ) * NORMS.after(kind, r))
                        if kind == "B0":
                            for n in range(NB):
                                pl.tensor_tensor(ctx_a[:, n * S:(n + 1) * S], ctx_a[:, n * S:(n + 1) * S],
                                                 table[:, n * S:(n + 1) * S], ALU.mult).then_inc(ctx_ready, 1)
                        else:
                            pl.tensor_tensor(ctx_b[:, :], ctx_b[:, :], rec_b[:, :], ALU.mult).then_inc(ctx_ready, 1)
                    if kind in PREPARES and k in (5, 6):
                        for n in {5: (0, 1), 6: (2, 3)}[k]:
                            g = 4 * PREPS.before(kind, r) + n
                            f, p = full[n % STAGES], parts[n % STAGES]
                            pool.wait_ge(prep_full, g + 1)
                            pl.tensor_tensor(f[:, :], f[:, :], p[:, 0, :], ALU.subtract).then_inc(parts_done, 1)
                            pool.wait_ge(parts_done, 3 * g + 1)
                            pl.tensor_tensor(p[:, 1, :], f[:, :], zeros[:, :], ALU.add).then_inc(parts_done, 1)
                            pool.wait_ge(parts_done, 3 * g + 2)
                            pl.tensor_tensor(p[:, 2, :], f[:, :], p[:, 1, :], ALU.subtract).then_inc(parts_done, 1)

            walk(pool, phase)
            for n in range(NB):
                pool.wait_ge(fin_stats, n + 1)
                pl.tensor_tensor(rstd[:, n * TB:(n + 1) * TB], rstd[:, n * TB:(n + 1) * TB],
                                 power[:, n * TB:(n + 1) * TB], ALU.pow).then_inc(fin_pow, 1)

        @block.scalar
        def _(act):
            for g in range(TT // 4):
                act.wait_ge(xt_ps, g + 1)
                nc.scalar.copy(srcT[:, g * CH:(g + 1) * CH], half[g]).then_inc(xt_sb, 1)

            def values_a(g):
                act.wait_ge(va_ps, g + 1)
                nc.scalar.copy(vtok_a[:, g * CH:(g + 1) * CH], half[g]).then_inc(va_sb, 1)

            def products(n):
                for w in range(3):
                    act.wait_ge(comp_ps, n + 1)
                    nc.scalar.activation(comp[:, (5 * n + w) * D:(5 * n + w + 1) * D],
                                         half[n % 4][:, w * D:(w + 1) * D], ACT.Copy,
                                         scale=ewb[:, 3 * n + w:3 * n + w + 1]).then_inc(comp_sb, 1)

            act.wait_ge(wb_in, 16 * 11)
            for n in range(2 * NB * NCH):
                act.wait_ge(rope_full, n + 1)
                need(act, a_written[n % STAGES], 3 * 16 * (n // STAGES))
                nc.scalar.copy(parts[n % STAGES][:, 0, :], full[n % STAGES][:, :]).then_inc(rope_hi, 1)
                act.wait_ge(rope_res, n + 1)
                nc.scalar.copy(parts[n % STAGES][:, 1, :], full[n % STAGES][:, :]).then_inc(rope_mid, 1)
                if n == 1:
                    for g in range(TT // 4):
                        values_a(g)
                if n >= 2:
                    products(n - 2)

            def phase(kind, r, c, b):
                ph = PHASES.before(kind, r)
                for k in range(STEPS[kind]):
                    u = UP * ph + k
                    for i in range(TB):
                        which = kind_at(kind, k, 2)
                        if which:
                            x0 = PIECES.before(kind, r) + piece_no(kind, k, i)
                            scale = (SCALE_A, SCALE_B)[which == "B"]
                            need(act, pv_done, TB * (u - 2) + i - RING + 1)
                            for n, (lo, hi) in enumerate(pieces(which, i)):
                                bank = (piece_no(kind, k, i) + n) % 2
                                act.wait_ge(s2_ready, x0 + n + 1)
                                nc.scalar.activation(probs[i % RING][:, lo:hi], s2[bank][:, 0:hi - lo], ACT.Exp,
                                                     scale=scale).then_inc(exp_done, 1)
                        if i == 0 and kind_at(kind, k, 3):
                            act.wait_ge(pv_done, TB * (u - 2))
                            need(act, ctx_out[(k - 3) % 2], 16 * ((UP // 2) * ph + (k - 3) // 2))
                            nc.scalar.copy(csb[(k - 3) % 2][:, :], cps[:, 0:GQ]).then_inc(ctx_sb, 1)
                        if i == MT_SLOT and kind_at(kind, k, 1):
                            act.wait_ge(mt_ready, u)
                            need(act, mrow_in[(k - 3) % RING], 16 * (2 * ph + (k - 3) // RING + 1)
                                 if kind_at(kind, k, 3) else 0)
                            nc.scalar.copy(mrows[(k - 1) % 2][:, :], misc_rows).then_inc(mrow_sb, 1)
                        if (k, i) in EXTRA[kind]:
                            extra(kind, r, c, b, ph, *EXTRA[kind][k, i])

            def extra(kind, r, c, b, ph, what, w):
                preps = PREPS.before(kind, r)
                steps = PREP_STEPS.before(kind, r) + (prep_no(kind, what, w) if what not in ("xa", "fin") else 0)
                if what == "node":
                    act.wait_ge(prep_ps, steps)
                    act.wait_ge(cur_ready, CUR_FIRST + CUR_COPIES.after(kind, r))
                    nc.scalar.activation(srcT[:, bass.ds(c * T + b * S + w * CH, CH)], misc[:, :], ACT.Identity,
                                         bias=cur_bias[:, 2:3]).then_inc(node_ready, 1)
                elif what in ("q", "k"):
                    n = 2 * (what == "k") + w
                    act.wait_ge(prep_ps, steps)
                    act.wait_ge(cur_ready, CUR_FIRST + CUR_COPIES.after(kind, r))
                    need(act, written, 4 * 3 * 16 * preps)
                    bias = cur_bias[:, (what == "k"):(what == "k") + 1]
                    nc.scalar.activation(full[n % STAGES][:, :], misc[:, :], ACT.Identity, bias=bias)
                    nc.scalar.activation(parts[n % STAGES][:, 0, :], misc[:, :], ACT.Identity, bias=bias
                                         ).then_inc(prep_full, 1)
                elif what == "v":
                    act.wait_ge(prep_ps, steps)
                    need(act, vs_ready, UP * ph)
                    nc.scalar.copy(vtok_b[:, bass.ds(b * TB * D + w * CH, CH)], misc[:, :]).then_inc(v_ready, 1)
                elif what == "fin":
                    act.wait_ge(fin_ps, w + 1)
                    nc.scalar.copy(fin[:, w * CH:(w + 1) * CH], misc[:, :]).then_inc(fin_sb, 1)

            walk(act, phase)
            for w in range(2):
                act.wait_ge(fin_ps, 2 + w + 1)
                nc.scalar.copy(fin[:, S + w * CH:S + (w + 1) * CH], misc[:, :]).then_inc(fin_sb, 1)

        @block.vector
        def _(dve):
            ve = nc.vector
            order = [0]

            def after(ins):
                order[0] += 1
                ins.then_inc(dve_order, 1)
                dve.wait_ge(dve_order, order[0])

            def moments(src, t0, tiles):
                for t in range(t0, t0 + tiles):
                    last = ve.bn_stats(stats[:, 6 * t:6 * t + 6], src[:, t * D:(t + 1) * D])
                after(last)
                for t in range(t0, t0 + tiles):
                    last = ve.bn_aggr(mv[:, 2 * t:2 * t + 2], stats[:, 6 * t:6 * t + 6])
                after(last)

            dve.wait_ge(x_in, 16 * NB)
            moments(xtok, 0, TT)
            ve.tensor_scalar_add(rstd[:, :], mv[:, 1:2 * TT:2], EPS_A).then_inc(ln_stats, 1)
            dve.wait_ge(ln_pow, 1)
            for t in range(TT):
                ve.tensor_scalar(xn[:, t * D:(t + 1) * D], xtok[:, t * D:(t + 1) * D], mv[:, 2 * t:2 * t + 1],
                                 rstd[:, t:t + 1], ALU.subtract, ALU.mult).then_inc(xn_ready, 1)

            def rest(n):
                dve.wait_ge(rope_hi, n + 1)
                ve.tensor_tensor(full[n % STAGES][:, :], full[n % STAGES][:, :], parts[n % STAGES][:, 0, :],
                                 ALU.subtract).then_inc(rope_res, 1)

            dve.wait_ge(wa_in, 16 * 7)
            for n in range(2 * NB * NCH):
                w, op = n // 2 % NCH, n % 2
                plain, swapped = ((s2[0], s2[1]), (cps, misc))[n % 2]
                dve.wait_ge(rot_ps, n + 1)
                need(dve, rope_full, n)
                ve.scalar_tensor_tensor(rope[0][:, :], plain[:, :], bias_a[:, 2 * op:2 * op + 1],
                                        table[:, w * CH:(w + 1) * CH], ALU.add, ALU.mult)
                ve.scalar_tensor_tensor(rope[1][:, :], swapped[:, :], bias_a[:, 2 * op + 1:2 * op + 2],
                                        table[:, S + w * CH:S + (w + 1) * CH], ALU.add, ALU.mult
                                        ).then_inc(rot_done, 1)
                dve.wait_ge(rot_done, n + 1)
                need(dve, a_low, n - STAGES + 1)
                ve.tensor_tensor(full[n % STAGES][:, :], rope[0][:, :], rope[1][:, :], ALU.add).then_inc(rope_full, 1)
                if n >= 1:
                    rest(n - 1)
            rest(2 * NB * NCH - 1)

            dve.wait_ge(wb_in, 16 * 11)
            for n in range(NODES):
                ve.tensor_scalar(comp[:, (5 * n + 3) * D:(5 * n + 4) * D], w4_sb[:, (3 * NODES + n) * D:(3 * NODES + n + 1) * D],
                                 actb[:, n:n + 1], None, ALU.mult)
                last = ve.tensor_scalar(comp[:, (5 * n + 4) * D:(5 * n + 5) * D], we_q_sb[:, n * D:(n + 1) * D],
                                        ewb[:, 3 * n:3 * n + 1], None, ALU.mult)
            last.then_inc(wo_ready, 1)
            dve.wait_ge(bias_ps, 1)
            ve.tensor_tensor(vbias[:, :], half[2][:, 0:3 * NODES], ewb[:, :], ALU.mult).then_inc(vbias_ready, 1)
            dve.wait_ge(vbias_ready, 1)
            after(ve.tensor_copy(bias_b[:, :], vbias[:, :]))
            after(ve.tensor_tensor(bias_b[:, 2:3 * NODES:3], be_sb[:, 0:3 * NODES:3], ewb[:, 0:3 * NODES:3], ALU.mult))
            dve.wait_ge(node_bias_ps, 1)
            ve.tensor_tensor(bias_b[:, 2:3 * NODES:3], half[2][:, 32:32 + NODES], bias_b[:, 2:3 * NODES:3],
                             ALU.add).then_inc(bias_done, 1)
            dve.wait_ge(row_ps, 1)
            ve.tensor_tensor(row_o[:, :], half[3][0:1, 0:128], row_o[:, :], ALU.add)
            ve.tensor_copy(row_n[:, :], half[3][0:1, 128:256]).then_inc(row_sb, 1)
            dve.wait_ge(spread_ps, 1)
            after(ve.tensor_tensor(lnb[:, :], half[3][:, 256:384], lnb[:, :], ALU.add))
            xt3 = xtok[:, :].rearrange("p (t d) -> p t d", d=D)
            ve.tensor_tensor(xt3, xt3, lnb[:, :].unsqueeze(1).broadcast_to([128, TT, D]), ALU.add).then_inc(pro_done, 1)
            dve.wait_ge(pro_done, 1)

            def phase(kind, r, c, b):
                ph = PHASES.before(kind, r)
                for k in range(STEPS[kind]):
                    u = UP * ph + k
                    for i in range(TB):
                        if kind != "T":
                            if i == 0:
                                need(dve, max_parts, 4 * (u - 1))
                            width = 128 * (i + 1) if kind[0] == "A" else S
                            dve.wait_ge(s1_ready, TB * u + i + 1)
                            ve.tensor_reduce(neg_max[k % 2][:, i:i + 1], s1[i % 2][:, 0:width], AX.X, ALU.max,
                                             negate=True).then_inc(max_done, 1)
                        if NORMS.per[kind] and (k, i) == ((2, 7) if kind == "T" else (3, 1)):
                            dve.wait_ge(sums_in, 16 * NORMS.after(kind, r))
                            cols = (HA if kind == "B0" else HB) * S // 128
                            for n in range(NORMS.per[kind]):
                                ve.reciprocal(sums[:, n * cols:(n + 1) * cols], sums[:, n * cols:(n + 1) * cols]
                                              ).then_inc(rec_ready, 1)
                        if EXTRA[kind].get((k, i), ("", 0))[0] == "xa":
                            g = EXTRA[kind][k, i][1]
                            dve.wait_ge(xa_ps, g + 1)
                            ve.tensor_tensor(xtok[:, g * CH:(g + 1) * CH], misc[:, :], xtok[:, g * CH:(g + 1) * CH],
                                             ALU.add).then_inc(xa_done, 1)

            def finish(n):
                dve.wait_ge(fin_sb, NCH * (n + 1))
                moments(fin, n * TB, TB)
                ve.tensor_scalar_add(rstd[:, n * TB:(n + 1) * TB], mv[:, 2 * n * TB + 1:2 * (n + 1) * TB:2], EPS_B
                                     ).then_inc(fin_stats, 1)
                dve.wait_ge(fin_pow, n + 1)
                for t in range(n * TB, (n + 1) * TB):
                    last = ve.tensor_scalar(fin[:, t * D:(t + 1) * D], fin[:, t * D:(t + 1) * D], mv[:, 2 * t:2 * t + 1],
                                            rstd[:, t:t + 1], ALU.subtract, ALU.mult)
                after(last)
                f3 = fin[:, n * S:(n + 1) * S].rearrange("p (t d) -> p t d", d=D)
                after(ve.tensor_tensor(f3, f3, lng[:, :].unsqueeze(1).broadcast_to([128, TB, D]), ALU.mult))
                ve.tensor_tensor(fin[:, n * S:(n + 1) * S], fin[:, n * S:(n + 1) * S], xtok[:, n * S:(n + 1) * S],
                                 ALU.add).then_inc(out_ready, 1)

            walk(dve, phase)
            for n in range(NB):
                finish(n)

        @block.tensor
        def _(pe):
            te = nc.tensor

            def mm(dst, lhsT, rhs, start=True, stop=True):
                return te.matmul(dst, lhsT, rhs, start=start, stop=stop)

            pe.wait_ge(pool_const, 4)
            for t in range(TT):
                pe.wait_ge(xn_ready, t + 1)
                last = te.transpose(half[t // 4][:, t % 4 * 128:(t % 4 + 1) * 128], xn[:, t * D:(t + 1) * D], ident[:, :])
                if t % 4 == 3:
                    last.then_inc(xt_ps, 1)

            def rotate(n):
                chunk, op = n // 2, n % 2
                src = srcT[:, chunk * CH:(chunk + 1) * CH]
                pe.wait_ge(xt_sb, chunk + 1)
                need(pe, rot_done, n - 1)
                for dst, w in zip(((s2[0], s2[1]), (cps, misc))[n % 2], (2 * op, 2 * op + 1)):
                    last = mm(dst[:, :], w_a[:, w * D:(w + 1) * D], src)
                last.then_inc(rot_ps, 1)

            def products(n):
                need(pe, va_sb, min(n + 1, 4))
                need(pe, comp_sb, 3 * (n - 3))
                for w in range(3):
                    last = mm(half[n % 4][:, w * D:(w + 1) * D], we_t_sb[:, (3 * n + w) * D:(3 * n + w + 1) * D],
                              w4_sb[:, (w * NODES + n) * D:(w * NODES + n + 1) * D])
                last.then_inc(comp_ps, 1)

            pe.wait_ge(wa_in, 16 * 7)
            rotate(0)
            rotate(1)
            for g in range(TT // 4):
                pe.wait_ge(xt_sb, g + 1)
                for t in range(4):
                    last = mm(half[g][:, t * D:(t + 1) * D], srcT[:, (4 * g + t) * D:(4 * g + t + 1) * D],
                              w_a[:, 4 * D:5 * D])
                last.then_inc(va_ps, 1)
            pe.wait_ge(wb_in, 16 * 11)
            for n in range(2, 2 * NB * NCH):
                rotate(n)
                products(n - 2)
            pe.wait_ge(comp_sb, 3 * NODES)
            for n in range(NODES):
                for w in range(3):
                    last = mm(half[2][:, 3 * n + w:3 * n + w + 1], w4_sb[:, (w * NODES + n) * D:(w * NODES + n + 1) * D],
                              be_sb[:, 3 * n + w:3 * n + w + 1])
            last.then_inc(bias_ps, 1)
            pe.wait_ge(vbias_ready, 1)
            pe.wait_ge(wo_ready, 1)
            for n in range(NODES):
                last = mm(half[2][:, 32 + n:33 + n], comp[:, (5 * n + 3) * D:(5 * n + 4) * D], vbias[:, 3 * n + 2:3 * n + 3])
            last.then_inc(node_bias_ps, 1)
            pe.wait_ge(bias_done, 1)
            mm(half[3][0:1, 0:128], bias_a[:, 4:5], w_a[:, 5 * D:6 * D])
            mm(half[3][0:1, 128:256], bias_b[:, 3 * NODES - 1:3 * NODES], ident[:, :]).then_inc(row_ps, 1)
            pe.wait_ge(row_sb, 1)
            pe.wait_ge(pool_const, N_CONST)
            mm(half[3][:, 256:384], ones_row[:, :], row_o[:, :]).then_inc(spread_ps, 1)
            pe.wait_ge(pro_done, 1)
            pe.wait_ge(rot_done, 2 * NB * NCH)

            def context(which, u, j, k, ph):
                pe.wait_ge(exp_done, context_need[0])
                if j == 0:
                    need(pe, ctx_sb, u)
                    pe.wait_ge(vs_ready, u + 1)
                q0 = 128 * j if which == "A" else 0
                for g in range(S // GQ):
                    lo, hi = max(g * GQ, q0), (g + 1) * GQ
                    if lo >= hi:
                        continue
                    last_j = 2 * g + 1 if which == "A" else TB - 1
                    last = te.matmul(cps[g * VW:(g + 1) * VW, lo - g * GQ:GQ], vs[k % RING][:, j, :],
                                     probs[j % RING][:, lo - q0:hi - q0], start=(j == 0), stop=(j == last_j),
                                     tile_position=(0, g * VW))
                last.then_inc(pv_done, 1)

            context_need = [0]

            def release(kind, r, what, w):
                preps = PREPS.before(kind, r)
                if what == "mt":
                    return mrow_sb, UP * PHASES.before(kind, r) + w
                if what == "node":
                    return node_ready, 2 * NODE_PHASES.before(kind, r) + w + 1
                if what in ("q", "k"):
                    return prep_full, 4 * preps + 2 * (what == "k") + w + 1
                if what == "v":
                    return v_ready, NCH * preps + w + 1
                return (xa_done, w + 1) if what == "xa" else (fin_sb, w + 1)

            def bank_free(kind, r, k, i, extra):
                uses = [(u, MT_SLOT, 0, "mt", u) for u in range(STEPS[kind]) if kind_at(kind, u, 1)]
                uses = sorted(uses + [(*at, 1, *v) for at, v in EXTRA[kind].items()])
                n = [x[:3] for x in uses].index((k, i, int(extra)))
                if n:
                    need(pe, *release(kind, r, *uses[n - 1][3:]))
                else:
                    need(pe, mrow_sb, UP * PHASES.before(kind, r) - 1)

            def extra(kind, r, c, b, what, w):
                cols = slice(w * CH, (w + 1) * CH)
                if what == "node":
                    pe.wait_ge(ctx_ready, NORMS.after(kind, r))
                    pe.wait_ge(cur_ready, CUR_FIRST + CUR_COPIES.after(kind, r))
                    mm(misc[:, :], cur[:, 2 * D:3 * D], ctx_b[:, cols], stop=False)
                    mm(misc[:, :], cur[:, 3 * D:4 * D], srcT[:, bass.ds((c - 1) * T + b * S + w * CH, CH)],
                       start=False).then_inc(prep_ps, 1)
                elif what in ("q", "k"):
                    op = int(what == "k")
                    need(pe, node_ready, 2 * NODE_PHASES.after(kind, r))
                    pe.wait_ge(cur_ready, CUR_FIRST + CUR_COPIES.after(kind, r))
                    at = (c // PREV if op else c) * T + b * S + w * CH
                    mm(misc[:, :], cur[:, op * D:(op + 1) * D], srcT[:, bass.ds(at, CH)]).then_inc(prep_ps, 1)
                elif what == "v":
                    pe.wait_ge(vsrc_in, 16 * PREPS.after(kind, r))
                    for t in range(4):
                        last = mm(misc[:, t * D:(t + 1) * D], vsrc[:, w * CH + t * 128:w * CH + (t + 1) * 128],
                                  comp[:, bass.ds(c * 5 * D + 2 * D, D)])
                    last.then_inc(prep_ps, 1)
                elif what == "xa":
                    pe.wait_ge(ctx_ready, NB)
                    for t in range(4):
                        last = mm(misc[:, t * D:(t + 1) * D], ctx_a[:, (4 * w + t) * 128:(4 * w + t + 1) * 128],
                                  w_a[:, 5 * D:6 * D])
                    last.then_inc(xa_ps, 1)
                else:
                    last_node(0, w, NORMS.after(kind, r))

            def last_node(batch, w, norms):
                pe.wait_ge(ctx_ready, norms)
                at = (5 * (NODES - 1)) * D
                for t in range(4 * w, 4 * w + 4):
                    dst, tok = misc[:, t % 4 * D:(t % 4 + 1) * D], slice(t * 128, (t + 1) * 128)
                    src = (NODES - 1) * T + batch * S + t * 128
                    mm(dst, ctx_b[:, tok], comp[:, at + 3 * D:at + 4 * D], stop=False)
                    mm(dst, srcT[:, src:src + 128], comp[:, at + 4 * D:at + 5 * D], start=False, stop=False)
                    last = mm(dst, ones_row[:, :], row_n[:, :], start=False)
                last.then_inc(fin_ps, 1)

            def phase(kind, r, c, b):
                ph = PHASES.before(kind, r)
                for k in range(STEPS[kind]):
                    u = UP * ph + k
                    which = kind_at(kind, k, 2)
                    for i in range(TB):
                        if which:
                            q, ky = qs[(k - 2) % RING], ks[(k - 2) % RING]
                            if i == 0:
                                pe.wait_ge(mrow_in[(k - 2) % RING], 16 * (2 * ph + (k - 2) // RING + 1))
                            q0 = 128 * i if which == "A" else 0
                            for n, (lo, hi) in enumerate(pieces(which, i)):
                                x0 = piece_no(kind, k, i) + n
                                bank = s2[x0 % 2]
                                need(pe, exp_done, PIECES.before(kind, r) + x0 - 1)
                                diagonal = which == "A" and n == 0
                                last = mm(bank[:, 0:hi - lo], ky[0:KALL, i * 128:(i + 1) * 128],
                                          q[0:KALL, q0 + lo:q0 + hi], stop=not diagonal)
                                if diagonal:
                                    last = mm(bank[:, 0:128], ident_h[:, :], mask_k[:, :], start=False)
                                last.then_inc(s2_ready, 1)
                        if kind != "T":
                            q, ky = qs[k % RING], ks[k % RING]
                            if i == 0:
                                pe.wait_ge(qk_in[k % RING], 32 * (2 * ph + k // RING + 1))
                            need(pe, max_done, TB * u + i - 1)
                            width = 128 * (i + 1) if kind[0] == "A" else S
                            for lo in range(0, width, CH):
                                hi = min(lo + CH, width)
                                diagonal = kind[0] == "A" and hi == width
                                last = mm(s1[i % 2][:, lo:hi], q[0:KROW, i * 128:(i + 1) * 128], ky[0:KROW, lo:hi],
                                          stop=not diagonal)
                                if diagonal:
                                    last = mm(s1[i % 2][:, width - 128:width], ident_h[:, :], mask_q[:, :], start=False)
                            last.then_inc(s1_ready, 1)
                        if i == 0 and kind_at(kind, k, 3):
                            context_need[0] = PIECES.before(kind, r) + pieces_before(kind, k)
                            context(kind_at(kind, k, 3), u - 3, TB - 1, k - 3, ph)
                        elif i > 0 and which:
                            context_need[0] = PIECES.before(kind, r) + piece_no(kind, k, i)
                            context(which, u - 2, i - 1, k - 2, ph)
                        if i == MT_SLOT and kind_at(kind, k, 1):
                            pe.wait_ge(max_parts, 4 * u)
                            bank_free(kind, r, k, i, False)
                            te.transpose(misc_rows, mparts[(k - 1) % 2][:, :], ident_h[:, :]).then_inc(mt_ready, 1)
                        if (k, i) in EXTRA[kind]:
                            bank_free(kind, r, k, i, True)
                            extra(kind, r, c, b, *EXTRA[kind][k, i])

            walk(pe, phase)
            for w in range(NCH):
                pe.wait_ge(fin_sb, NCH + w)
                last_node(1, w, NORMS.after("T", 0))


def rotation_tables():
    import numpy as np

    half = DA // 2
    inv = (1.0 / np.float32(10000.0) ** (np.arange(half, dtype=np.float32) / np.float32(half))).astype(np.float32)
    angles = np.outer(np.arange(S, dtype=np.float32), inv).astype(np.float32)
    cos, sin = np.cos(angles).T, np.sin(angles).T
    cos = np.tile(np.concatenate([cos, cos]), (HA, 1))
    sin = np.tile(np.concatenate([-sin, sin]), (HA, 1))
    return np.ascontiguousarray(cos, dtype=np.float32), np.ascontiguousarray(sin, dtype=np.float32)


def kernel(**inputs):
    import numpy as np
    import concourse.bacc as bacc
    from concourse.bass_utils import run_bass_kernel_spmd as run

    a = {k.replace("L0_", ""): np.asarray(v) for k, v in inputs.items()}
    swap = np.arange(D).reshape(HA, 2, DA // 2)[:, ::-1].reshape(-1)
    w, bias = a["attn_qkv_w"], a["attn_qkv_b"]
    wq_a, wk_a, wv_a = w[0:D], w[D:2 * D], w[2 * D:3 * D]
    bq_a, bk_a, bv_a = bias[0:D], bias[D:2 * D], bias[2 * D:3 * D]
    order = np.array([e for node, _ in edges() for e in node])
    cos, sin = rotation_tables()
    arrays = {
        "x": a["attn_x"].reshape(T, D),
        "w_qk": np.concatenate([wq_a.T, wq_a[swap].T, wk_a.T, wk_a[swap].T], axis=1),
        "w_va": wv_a.T, "w_oa": a["attn_out_w"].T,
        "b_a": np.stack([bq_a, bq_a[swap], bk_a, bk_a[swap], bv_a], axis=1),
        "out_b": a["attn_out_b"].reshape(1, D),
        "cos": cos, "sin": sin,
        "ew": a["ffn_ew"].reshape(1, -1), "act_w": a["ffn_act_w"].reshape(1, -1),
        "we_t": a["ffn_We"][order].transpose(2, 0, 1).reshape(D, -1),
        "we_q": a["ffn_We"][order[0::3]],
        "be": a["ffn_be"][order].T,
        "wq": a["ffn_Wq"], "wk": a["ffn_Wk"], "wv": a["ffn_Wv"], "wo": a["ffn_Wo"],
        "ln_g": a["ffn_ln_g"].reshape(1, D), "ln_b": a["ffn_ln_b"].reshape(1, D),
    }
    arrays = {k: np.ascontiguousarray(v) for k, v in arrays.items()}
    nc = bacc.Bacc("TRN2", target_bir_lowering=False, num_devices=1)
    args = [nc.dram_tensor(f"in_{k}", v.shape, mybir.dt.from_np(v.dtype), kind="ExternalInput").ap()
            for k, v in arrays.items()]
    out = nc.dram_tensor("out", (T, D), F32, kind="ExternalOutput").ap()
    dual_attention_kernel(nc, *args, out)
    r = run(nc, [{f"in_{k}": v for k, v in arrays.items()}], core_ids=[0])
    return r.results[0]["out"].reshape(NB, S, D)
```

```python
import concourse.bass as bass
from concourse import mybir
from contextlib import ExitStack

F32 = mybir.dt.float32
BF16 = mybir.dt.bfloat16
ACT = mybir.ActivationFunctionType
ALU = mybir.AluOpType
AX = mybir.AxisListType

D = 128
NB, S = 2, 1024
T = NB * S
TT = T // 128
TB = S // 128
CH = 512
NCH = S // CH
HA, DA = 16, 8
HB, DB = 8, 16
NODES, PREV = 6, 5
UP = 8
RING = 4
STAGES = 4
KROW = 96
MROW = KROW
KALL = KROW + 3
GQ = 256
VW = 32
LROW = 16
SCALE_A, SCALE_B = DA ** -0.5, DB ** -0.5
EPS_A, EPS_B = 1e-5, 1e-6
MASKED = -1e30
Q_ROWS = [(0, 3, 1), (3, 6, 2), (4, 5, 1)]
K_ROWS = [(2, 5, 1), (1, 6, 4), (0, 1, 1)]


def edges():
    first, out = 0, []
    for c in range(NODES):
        n = min(c + 1, PREV)
        out.append(((first + n - 1, first, first + n // 2), (c, c - n + 1, c - n + 1 + n // 2)))
        first += n
    return out


KEY_TILES = {"A": [[0], [1, 7], [2, 6], [3, 5], [4]], "B": [[j] for j in range(TB)]}
N_TILES = {kind: len(KEY_TILES[kind]) for kind in "AB"}
N_PROBS = {"A": 5, "B": 4}
MT_SLOT = {"A": 1, "B": 3}


def key_tiles(kind, i):
    out, at = [], 0
    for j in KEY_TILES[kind][i]:
        q0 = 128 * j if kind == "A" else 0
        out.append((j, at, q0))
        at += S - q0
    return out


def query_tiles(kind, i):
    if kind == "B":
        return [(i, 0, S)]
    return [(TB - 1 - j, at, at + S - q0) for j, at, q0 in key_tiles(kind, i)]


def width(kind, i):
    return query_tiles(kind, i)[-1][2]


def pieces(kind, i):
    return [(lo, min(lo + CH, width(kind, i))) for lo in range(0, width(kind, i), CH)]


def last_tile(kind, g):
    return [j for tiles in KEY_TILES[kind] for j in tiles if kind == "B" or 128 * j < GQ * (g + 1)][-1]


N_PIECES = {k: sum(len(pieces(k, j)) for j in range(N_TILES[k])) for k in "AB"}
NODE_AT = {(4, 1): ("node", 0), (4, 5): ("node", 1)}
PREP_AT = {(4, 7): ("q", 0), (5, 1): ("q", 1), (5, 5): ("k", 0), (5, 7): ("k", 1),
           (6, 1): ("v", 0), (6, 5): ("v", 1)}
PREP_A_AT = {(4, 3): ("q", 0), (5, 0): ("q", 1), (5, 3): ("k", 0), (6, 0): ("k", 1),
             (6, 3): ("v", 0), (7, 0): ("v", 1)}
XA_AT = {(1, 1): ("xa", 0), (1, 5): ("xa", 1), (2, 1): ("xa", 2), (2, 5): ("xa", 3)}
FIN_AT = {(4, 1): ("fin", 0), (4, 5): ("fin", 1)}

KINDS = ["A0", "AL", "AZ", "B0", "BL", "BE", "T"]
TIMES = {"A0": 1, "AL": NB * HA // UP - 2, "AZ": 1, "B0": 1, "BL": (NODES - 1) * NB, "BE": 1, "T": 1}
EXTRA = {"A0": PREP_A_AT, "AL": {}, "AZ": {}, "B0": PREP_AT, "BL": {**NODE_AT, **PREP_AT},
         "BE": {**XA_AT, **FIN_AT}, "T": {}}
PREPARES = ("A0", "B0", "BL")
STEPS = {k: 3 if k == "T" else UP for k in KINDS}
TURNS = {k: N_TILES["A"] if k[0] == "A" else TB for k in KINDS}


def which_turns(kind):
    return "A" if kind[0] == "A" else "B"


def kind_at(kind, k, lag):
    if k - lag >= 0:
        return None if kind == "T" else kind[0]
    return {"A0": None, "AL": "A", "AZ": "A", "B0": "A", "BL": "B", "BE": "B", "T": "B"}[kind]


class Count:

    def __init__(self, **per):
        self.per = {k: per.get(k, 0) for k in KINDS}

    def before(self, kind, r):
        n = sum(self.per[x] * TIMES[x] for x in KINDS[:KINDS.index(kind)])
        return n + r * self.per[kind] if TIMES[kind] > 1 and self.per[kind] else n

    def after(self, kind, r):
        return self.before(kind, r) + self.per[kind]


def pieces_before(kind, k):
    return sum(N_PIECES[kind_at(kind, u, 2)] for u in range(k) if kind_at(kind, u, 2))


def steps_before(kind, k, lag):
    return sum(N_TILES[kind_at(kind, u, lag)] for u in range(k) if kind_at(kind, u, lag))


PHASES = Count(A0=1, AL=1, AZ=1, B0=1, BL=1, BE=1)
PIECES = Count(**{k: pieces_before(k, STEPS[k]) for k in KINDS})
MAXIMA = Count(**{k: steps_before(k, UP, 0) for k in KINDS if k != "T"})
ADDED = Count(**{k: steps_before(k, STEPS[k], 2) for k in KINDS})
PREPS = Count(A0=1, B0=1, BL=1)
PREP_STEPS = Count(**{k: len(EXTRA[k]) for k in ("A0", "BL")}, B0=len(PREP_AT))
NODE_PHASES = Count(BL=1)
NORMS = Count(B0=NB, BL=1, BE=1, T=1)
CUR_COPIES = Count(BL=4)
CUR_FIRST = 2
N_CONST = 10 + 5 * RING


def added(kind, r, k):
    if k < -3:
        return ADDED.before(kind, r) - (N_TILES[kind_at(kind, 0, 3)] if kind_at(kind, 0, 3) else 0)
    return ADDED.before(kind, r) + steps_before(kind, k + 3, 2)


def piece_no(kind, k, j):
    which = kind_at(kind, k, 2)
    return pieces_before(kind, k) + sum(len(pieces(which, t)) for t in range(j))


def prep_no(kind, what, w):
    steps = [v for _, v in sorted(EXTRA[kind].items()) if v[0] != "xa"]
    return steps.index((what, w)) + 1


def dual_attention_kernel(nc, x, w_qk, w_va, w_oa, b_a, out_b, cos, sin, ew, act_w, we_t, we_q,
                          be, wq, wk, wv, wo, ln_g, ln_b, out):
    ctx = ExitStack()
    with ctx:
        def sb(name, shape, dt=F32):
            return ctx.enter_context(nc.sbuf_tensor(name, shape, dt))

        def pb(name, shape, dt=F32):
            return ctx.enter_context(nc.psum_tensor(name, shape, dt))

        def sem(name):
            return ctx.enter_context(nc.semaphore(name))

        qk_dram = {"A": nc.dram_tensor("dram_qk_a", (2, 6, NB * HA * DA, S), BF16).ap(),
                   "B": nc.dram_tensor("dram_qk_b", (2, 6, NB * HB * DB, S), BF16).ap()}
        raw_dram = {"A": nc.dram_tensor("dram_raw_a", (NB * HA, 128, GQ), F32).ap(),
                    "B": nc.dram_tensor("dram_raw_b", (NB * HB, 128, GQ), F32).ap()}
        rec_dram = {"A": nc.dram_tensor("dram_rec_a", (NB, HA, S), F32).ap(),
                    "B": nc.dram_tensor("dram_rec_b", (NB, HB, S), F32).ap()}

        srcT = sb("srcT", [128, NODES * T])
        xtok = sb("xtok", [128, TT * D])
        qs = [sb(f"qs{s}", [128, S], BF16) for s in range(RING)]
        ks = [sb(f"ks{s}", [128, S], BF16) for s in range(RING)]
        vs = [sb(f"vs{s}", [128, TB, VW]) for s in range(RING)]
        probs = [sb(f"probs{s}", [128, S]) for s in range(N_PROBS["B"])]
        vtok_a = sb("vtok_a", [128, TT * D])
        vtok_b = sb("vtok_b", [128, NB * TB * D])
        comp = sb("comp", [128, NODES * 5 * D])
        cur = sb("cur", [128, 4 * D])
        cur_bias = sb("cur_bias", [128, 3])
        bias_b = sb("bias_b", [128, NODES * 3])
        w_a = sb("w_a", [128, 6 * D])
        bias_a = sb("bias_a", [128, 5])
        ctx_a = sb("ctx_a", [128, T])
        table = sb("table", [128, 2 * S])
        ctx_b = sb("ctx_b", [128, S])
        rec_b = sb("rec_b", [128, S])
        vsrc = sb("vsrc", [128, S])
        full = [sb(f"full{s}", [128, CH]) for s in range(STAGES)]
        parts = [sb(f"parts{s}", [128, 3, CH], BF16) for s in range(STAGES)]
        csb = [sb(f"csb{s}", [128, GQ]) for s in range(2)]
        neg_max = [sb(f"neg_max{s}", [128, TB]) for s in range(2)]
        mres = sb("mres", [128, TB])
        mparts = [sb(f"mparts{s}", [128, 3 * TB], BF16) for s in range(2)]
        mrows = [sb(f"mrows{s}", [3 * TB, 128], BF16) for s in range(2)]
        sums = sb("sums", [128, 4 * 64])
        rope = [sb(f"rope{s}", [128, CH]) for s in range(2)]
        ident = sb("ident", [128, 128])
        ident_h = sb("ident_h", [128, 128], BF16)
        mask_q = sb("mask_q", [128, 128], BF16)
        mask_k = sb("mask_k", [128, 128], BF16)
        ones_row = sb("ones_row", [1, 128])
        ewb = sb("ewb", [128, NODES * 3])
        actb = sb("actb", [128, NODES])
        be_sb = sb("be_sb", [128, NODES * 3])
        vbias = sb("vbias", [128, NODES * 3])
        row_o = sb("row_o", [1, 128])
        row_n = sb("row_n", [1, 128])
        lng = sb("lng", [128, D])
        lnb = sb("lnb", [128, D])
        stats = sb("stats", [128, TT * 6])
        mv = sb("mv", [128, TT * 2])
        rstd = sb("rstd", [128, TT])
        power = sb("power", [128, TT])
        zeros = sb("zeros", [128, CH])
        fin = sb("fin", [128, T])

        raw_w = srcT[:, 2 * T:5 * T]
        we_t_sb = raw_w[:, 0:NODES * 3 * D]
        we_q_sb = raw_w[:, NODES * 3 * D:NODES * 4 * D]
        w4_sb = raw_w[:, NODES * 4 * D:NODES * 8 * D]
        xn = fin
        exps = {"B": probs, "A": probs + [rec_b]}

        s1 = [pb(f"s1_{n}", [128, S]) for n in range(2)]
        s2 = [pb(f"s2_{n}", [128, CH]) for n in range(2)]
        cps = pb("cps", [128, CH])
        misc = pb("misc", [128, CH])

        sems = ("x_in wa_in wb_in pool_const ln_stats ln_pow xn_ready xt_ps xt_sb dve_order rot_ps rot_done "
                "rope_full rope_hi rope_res rope_mid a_low va_ps va_sb comp_ps comp_sb wo_ready bias_ps vbias_ready "
                "node_bias_ps bias_done row_ps row_sb spread_ps pro_done cur_ready s1_ready max_done max_parts "
                "mt_ready mrow_sb s2_ready exp_done pv_done ctx_sb vs_ready prep_ps prep_full parts_done v_ready "
                "node_ready vsrc_in sums_in ctx_in rec_ready rec_out rec_in ctx_ready xa_ps xa_done fin_ps fin_sb "
                "fin_stats fin_pow out_ready stored")
        (x_in, wa_in, wb_in, pool_const, ln_stats, ln_pow, xn_ready, xt_ps, xt_sb, dve_order, rot_ps, rot_done,
         rope_full, rope_hi, rope_res, rope_mid, a_low, va_ps, va_sb, comp_ps, comp_sb, wo_ready, bias_ps,
         vbias_ready, node_bias_ps, bias_done, row_ps, row_sb, spread_ps, pro_done, cur_ready, s1_ready, max_done,
         max_parts, mt_ready, mrow_sb, s2_ready, exp_done, pv_done, ctx_sb, vs_ready, prep_ps, prep_full,
         parts_done, v_ready, node_ready, vsrc_in, sums_in, ctx_in, rec_ready, rec_out, rec_in, ctx_ready, xa_ps,
         xa_done, fin_ps, fin_sb, fin_stats, fin_pow, out_ready, stored) = [sem(n) for n in sems.split()]
        qk_in = [sem(f"qk_in{n}") for n in range(RING)]
        mrow_in = [sem(f"mrow_in{n}") for n in range(RING)]
        ctx_out = [sem(f"ctx_out{n}") for n in range(2)]
        written = sem("written")
        a_written = [sem(f"a_written{n}") for n in range(STAGES)]
        half = [s1[n // 2][:, n % 2 * CH:(n % 2 + 1) * CH] for n in range(4)]
        misc_rows = misc[0:3 * TB, 0:64].bitcast(BF16)

        def need(eng, s, value):
            if isinstance(value, int) and value <= 0:
                return
            eng.wait_ge(s, value)

        def walk(eng, phase):
            phase("A0", 0, 0, 0)
            with eng.Fori(0, TIMES["AL"]) as r:
                phase("AL", r, 0, 0)
            phase("AZ", 0, 0, 0)
            phase("B0", 0, 0, 1)
            with eng.Fori(1, NODES) as c:
                with eng.Fori(0, NB) as b:
                    phase("BL", (c - 1) * NB + b, c, b)
            phase("BE", 0, 0, 0)
            phase("T", 0, 0, 1)

        def head_row(kind, r, k, b):
            if kind[0] == "A" or kind == "B0" and k < 0:
                return {"A0": 0, "AL": r * UP + UP, "AZ": 3 * UP, "B0": 4 * UP}[kind] + k
            here = {"B0": 0, "BL": b * -1 + 1, "BE": 1, "T": 0}[kind]
            other = {"B0": 1, "BL": b, "BE": 0, "T": 1}[kind]
            return here * HB + k if 0 <= k < UP else other * HB + k % UP

        block = ctx.enter_context(nc.Block())

        @block.sync
        def _(sp):
            xt = x.rearrange("(t p) d -> p t d", p=128)
            for h in range(NB):
                sp.dma_start(xtok[:, h * S:(h + 1) * S].rearrange("p (t d) -> p t d", d=D),
                             xt[:, h * TB:(h + 1) * TB, :]).then_inc(x_in, 16)
            sp.dma_start(w_a[:, 0:4 * D], w_qk).then_inc(wa_in, 16)
            sp.dma_start(w_a[:, 4 * D:5 * D], w_va).then_inc(wa_in, 16)
            sp.dma_start(w_a[:, 5 * D:6 * D], w_oa).then_inc(wa_in, 16)
            sp.dma_start(bias_a[:, :], b_a).then_inc(wa_in, 16)
            sp.dma_start(table[:, 0:S], cos).then_inc(wa_in, 16)
            sp.dma_start(table[:, S:2 * S], sin).then_inc(wa_in, 16)
            sp.dma_start(row_o[:, :], out_b).then_inc(wa_in, 16)
            sp.dma_start(ewb[:, :], ew.partition_broadcast(128)).then_inc(wb_in, 16)
            sp.dma_start(actb[:, :], act_w.partition_broadcast(128)).then_inc(wb_in, 16)
            sp.dma_start(be_sb[:, :], be).then_inc(wb_in, 16)
            sp.dma_start(we_t_sb, we_t).then_inc(wb_in, 16)
            sp.dma_start(we_q_sb.rearrange("p (n d) -> p n d", n=NODES),
                         we_q.rearrange("n p d -> p n d")).then_inc(wb_in, 16)
            for n, w in enumerate((wq, wk, wv, wo)):
                sp.dma_start(w4_sb[:, n * NODES * D:(n + 1) * NODES * D].rearrange("p (n d) -> p n d", n=NODES),
                             w.rearrange("n p d -> p n d")).then_inc(wb_in, 16)
            sp.dma_start(lng[:, :], ln_g.partition_broadcast(128)).then_inc(wb_in, 16)
            sp.dma_start(lnb[:, :], ln_b.partition_broadcast(128)).then_inc(wb_in, 16)

            def write_parts(which, n, rows, op, w, done):
                for part, (lo, hi, step) in enumerate((Q_ROWS, K_ROWS)[op]):
                    groups = len(range(lo, hi, step))
                    sp.dma_start(qk_dram[which][op, lo:hi:step, rows, w * CH:(w + 1) * CH
                                                ].rearrange("r p s -> p r s"),
                                 parts[n % STAGES][:, part:part + 1, :].broadcast_to([128, groups, CH])
                                 ).then_inc(done, 16)

            n = 0
            for b in range(NB):
                for w in range(NCH):
                    for op in range(2):
                        sp.wait_ge(a_low, n + 1)
                        write_parts("A", n, slice(b * 128, (b + 1) * 128), op, w, a_written[n % STAGES])
                        n += 1
            for s in a_written:
                sp.wait_ge(s, 3 * 16 * n // STAGES)

            def load_unit(kind, r, k, b):
                which = "B" if kind[0] == "B" or (kind, k) == ("AZ", UP) else "A"
                row = 0 if (kind, k) == ("AZ", UP) else head_row(kind, r, k, b)
                dims, slot = (DA, DB)[which == "B"], k % RING
                if k < UP:
                    need(sp, pv_done, added(kind, r, k - RING))
                else:
                    sp.wait_ge(written, 4 * 3 * 16 * PREPS.after(kind, r))
                for op, dst in ((0, qs[slot]), (1, ks[slot])):
                    sp.dma_start(dst[0:6 * dims, :],
                                 qk_dram[which][op, :, bass.ds(row * dims, dims), :]
                                 ).then_inc(qk_in[slot], 16)

            sp.wait_ge(pool_const, N_CONST)
            load_unit("A0", 0, 0, 0)

            def norm_batches(kind, b):
                return {"B0": [0, 1], "BL": [b], "BE": [0], "T": [1]}.get(kind, [])

            def read_contexts(kind, r, b):
                which, heads, width = ("A", HA, DA) if kind == "B0" else ("B", HB, DB)
                cols = heads * S // 128
                for n, batch in enumerate(norm_batches(kind, b)):
                    raw = raw_dram[which][bass.ds(batch * heads, heads), :, :]
                    sp.dma_start(sums[:, n * cols:(n + 1) * cols],
                                 raw[:, LROW:128:VW, :].rearrange("h g (a n) -> h g a n", n=cols)
                                 ).then_inc(sums_in, 16)
                    dst = ctx_a[:, n * S:(n + 1) * S] if which == "A" else ctx_b
                    for g in range(S // GQ):
                        sp.dma_start(dst[:, g * GQ:(g + 1) * GQ], raw[:, g * VW:g * VW + width, :]
                                     ).then_inc(ctx_in, 16)

            def spread_reciprocals(kind, r, b):
                which, heads, width = ("A", HA, DA) if kind == "B0" else ("B", HB, DB)
                cols = heads * S // 128
                sp.wait_ge(rec_ready, NORMS.after(kind, r))
                for n, batch in enumerate(norm_batches(kind, b)):
                    sp.dma_start(rec_dram[which][bass.ds(batch, 1), :, :].rearrange("o h (a n) -> (o h a) n", n=cols),
                                 sums[:, n * cols:(n + 1) * cols]).then_inc(rec_out, 16)
                sp.wait_ge(rec_out, 16 * NORMS.after(kind, r))
                for n, batch in enumerate(norm_batches(kind, b)):
                    dst = table[:, n * S:(n + 1) * S] if which == "A" else rec_b[:, :]
                    src = rec_dram[which][bass.ds(batch, 1), :, :].rearrange("o h n -> (o h) n")
                    sp.dma_start(dst, src.unsqueeze(1).broadcast_to([heads, width, S])).then_inc(rec_in, 16)

            def phase(kind, r, c, b):
                ph = PHASES.before(kind, r)
                for k in range(STEPS[kind]):
                    u = UP * ph + k
                    if k < UP - 1 and kind != "T":
                        load_unit(kind, r, k + 1, b)
                    if kind_at(kind, k, 3):
                        sp.wait_ge(ctx_sb, u - 2)
                        sp.dma_start(raw_dram[kind_at(kind, k, 3)][bass.ds(head_row(kind, r, k - 3, b), 1), :, :
                                                                   ].rearrange("o p n -> (o p) n"),
                                     csb[(k - 3) % 2][:, :]).then_inc(ctx_out[(k - 3) % 2], 16)
                    if NORMS.per[kind] and k == 2:
                        for s in ctx_out:
                            sp.wait_ge(s, 16 * (UP // 2) * ph)
                        sp.wait_ge(prep_ps, PREP_STEPS.before(kind, r))
                        if kind == "T":
                            sp.wait_ge(fin_ps, 2)
                        read_contexts(kind, r, b)
                    if NORMS.per[kind] and k == (2 if kind == "T" else 3):
                        spread_reciprocals(kind, r, b)
                    if kind_at(kind, k, 1):
                        sp.wait_ge(mrow_sb, u)
                        sp.dma_start(qs[(k - 1) % RING][MROW:KALL, :].rearrange("a (i n) -> a i n", n=128),
                                     mrows[(k - 1) % 2][:, :]).then_inc(mrow_in[(k - 1) % RING], 16)
                    if kind in PREPARES and k == 5:
                        need(sp, node_ready, 2 * NODE_PHASES.after(kind, r))
                        need(sp, prep_ps, PREP_STEPS.before(kind, r))
                        sp.dma_start(vsrc[:, :], srcT[:, bass.ds((c + 1) // 2 * T + b * S, S)]
                                     ).then_inc(vsrc_in, 16)
                    if kind in PREPARES and k in (5, 6):
                        for n in {5: (0, 1), 6: (2, 3)}[k]:
                            sp.wait_ge(parts_done, 3 * (4 * PREPS.before(kind, r) + n + 1))
                            write_parts("B", n, bass.ds(b * 128, 128), n // 2, n % 2, written)
                    if k == UP - 1 and kind not in ("BE", "T"):
                        load_unit(kind, r, UP, b)

            walk(sp, phase)
            for b in range(NB):
                sp.wait_ge(out_ready, b + 1)
                sp.dma_start(out.rearrange("(t p) d -> p t d", p=128)[:, b * TB:(b + 1) * TB, :],
                             fin[:, b * S:(b + 1) * S].rearrange("p (t d) -> p t d", d=D)).then_inc(stored, 16)
            sp.wait_ge(stored, 16 * NB)
            for s in ctx_out:
                sp.wait_ge(s, 16 * UP // 2 * (NB * HA // UP + NODES * NB))
            sp.wait_ge(written, 4 * 3 * 16 * NODES * NB)
            sp.wait_ge(rec_out, 16 * NORMS.after("T", 0))

        @block.gpsimd
        def _(pool):
            pl = nc.gpsimd
            pl.memset(ident[:, :], 0.0).then_inc(pool_const, 1)
            pl.memset(mask_q[:, :], 0.0).then_inc(pool_const, 1)
            pl.memset(mask_k[:, :], 0.0).then_inc(pool_const, 1)
            pool.wait_ge(pool_const, 3)
            pl.affine_select(out=ident[:, :], in_=ident[:, :], pattern=[[-1, 128]], compare_op=ALU.not_equal,
                             fill=1.0, base=0, channel_multiplier=1).then_inc(pool_const, 1)
            pl.memset(power[:, :], -0.5).then_inc(pool_const, 1)
            pool.wait_ge(pool_const, 5)
            pl.tensor_copy(ident_h[:, :], ident[:, :]).then_inc(pool_const, 1)
            pool.wait_ge(ln_stats, 1)
            pl.tensor_tensor(rstd[:, :], rstd[:, :], power[:, :], ALU.pow).then_inc(ln_pow, 1)
            pl.affine_select(out=mask_q[:, :], in_=mask_q[:, :], pattern=[[-1, 128]], compare_op=ALU.is_ge,
                             fill=MASKED, base=0, channel_multiplier=1).then_inc(pool_const, 1)
            pl.affine_select(out=mask_k[:, :], in_=mask_k[:, :], pattern=[[1, 128]], compare_op=ALU.is_ge,
                             fill=MASKED, base=0, channel_multiplier=-1).then_inc(pool_const, 1)
            pl.memset(ones_row[:, :], 1.0).then_inc(pool_const, 1)
            pl.memset(zeros[:, :], 0.0).then_inc(pool_const, 1)
            for s in range(RING):
                pl.memset(qs[s][:, :], 0.0).then_inc(pool_const, 1)
                pl.memset(ks[s][:, :], 0.0).then_inc(pool_const, 1)
                pl.memset(vs[s][:, :, :], 0.0).then_inc(pool_const, 1)
            pool.wait_ge(pool_const, N_CONST - 2 * RING)
            for s in range(RING):
                pl.memset(vs[s][:, :, LROW:LROW + 1], 1.0).then_inc(pool_const, 1)
            for s in range(RING):
                pool.wait_ge(pool_const, N_CONST - RING + s)
                pl.memset(ks[s][MROW:128, :], 1.0).then_inc(pool_const, 1)
            pool.wait_ge(pool_const, N_CONST)
            for n in range(2 * NB * NCH):
                pool.wait_ge(rope_mid, n + 1)
                pl.tensor_tensor(parts[n % STAGES][:, 2, :], full[n % STAGES][:, :], parts[n % STAGES][:, 1, :],
                                 ALU.subtract).then_inc(a_low, 1)
            pool.wait_ge(comp_sb, 3 * NODES)
            pool.wait_ge(bias_done, 1)
            pl.tensor_copy(cur[:, 0:2 * D], comp[:, 0:2 * D]).then_inc(cur_ready, 1)
            pl.tensor_copy(cur_bias[:, 0:2], bias_b[:, 0:2]).then_inc(cur_ready, 1)

            def phase(kind, r, c, b):
                ph = PHASES.before(kind, r)
                for k in range(STEPS[kind]):
                    u = UP * ph + k
                    if kind_at(kind, k, 1):
                        v, nm, mp = u - 1, neg_max[(k - 1) % 2], mparts[(k - 1) % 2]
                        pool.wait_ge(max_done, MAXIMA.before(kind, r) + (steps_before(kind, k, 0) if k else 0))
                        need(pool, mt_ready, v - 1)
                        pl.tensor_tensor(mp[:, 0:TB], nm[:, :], zeros[:, 0:TB], ALU.add).then_inc(max_parts, 1)
                        pool.wait_ge(max_parts, 4 * v + 1)
                        pl.tensor_tensor(mres[:, :], nm[:, :], mp[:, 0:TB], ALU.subtract).then_inc(max_parts, 1)
                        pool.wait_ge(max_parts, 4 * v + 2)
                        pl.tensor_tensor(mp[:, TB:2 * TB], mres[:, :], zeros[:, 0:TB], ALU.add).then_inc(max_parts, 1)
                        pool.wait_ge(max_parts, 4 * v + 3)
                        pl.tensor_tensor(mp[:, 2 * TB:3 * TB], mres[:, :], mp[:, TB:2 * TB],
                                         ALU.subtract).then_inc(max_parts, 1)
                    if kind != "T":
                        which = kind[0]
                        dims = (DA, DB)[which == "B"]
                        batch = {"A0": 0, "AL": r, "AZ": 1, "B0": 0, "BL": b * -1 + 1, "BE": 1}[kind]
                        head = {"AL": (r * -1 + 1) * UP, "AZ": UP}.get(kind, 0) + k
                        need(pool, pv_done, added(kind, r, k - RING))
                        if kind == "A0" and k == 0:
                            pool.wait_ge(va_sb, TT // 4)
                        if which == "B":
                            pool.wait_ge(v_ready, NCH * PREPS.before(kind, r) if kind != "B0" else NCH)
                        src = (vtok_a, vtok_b)[which == "B"][:, :].rearrange("p (t d) -> p t d", d=D)
                        pl.tensor_copy(vs[k % RING][:, :, 0:dims],
                                       src[:, bass.ds(batch * TB, TB), bass.ds(head * dims, dims)]
                                       ).then_inc(vs_ready, 1)
                    if kind == "BL" and k == 0:
                        pool.wait_ge(mrow_sb, u - 1)
                        pl.tensor_tensor(cur[:, 0:2 * D], comp[:, bass.ds(c * 5 * D, 2 * D)], zeros[:, 0:2 * D],
                                         ALU.add).then_inc(cur_ready, 1)
                        pl.tensor_copy(cur[:, 2 * D:4 * D], comp[:, bass.ds(c * 5 * D - 2 * D, 2 * D)]
                                       ).then_inc(cur_ready, 1)
                        pl.tensor_copy(cur_bias[:, 0:2], bias_b[:, bass.ds(c * 3, 2)]).then_inc(cur_ready, 1)
                        pl.tensor_copy(cur_bias[:, 2:3], bias_b[:, bass.ds(c * 3 - 1, 1)]).then_inc(cur_ready, 1)
                    if NORMS.per[kind] and k == (2 if kind == "T" else 3):
                        pool.wait_ge(rec_in, 16 * NORMS.after(kind, r))
                        pool.wait_ge(ctx_in, 16 * (S // GQ) * NORMS.after(kind, r))
                        if kind == "B0":
                            for n in range(NB):
                                pl.tensor_tensor(ctx_a[:, n * S:(n + 1) * S], ctx_a[:, n * S:(n + 1) * S],
                                                 table[:, n * S:(n + 1) * S], ALU.mult).then_inc(ctx_ready, 1)
                        else:
                            pl.tensor_tensor(ctx_b[:, :], ctx_b[:, :], rec_b[:, :], ALU.mult).then_inc(ctx_ready, 1)
                    if kind in PREPARES and k in (5, 6):
                        for n in {5: (0, 1), 6: (2, 3)}[k]:
                            g = 4 * PREPS.before(kind, r) + n
                            f, p = full[n % STAGES], parts[n % STAGES]
                            pool.wait_ge(prep_full, g + 1)
                            pl.tensor_tensor(f[:, :], f[:, :], p[:, 0, :], ALU.subtract).then_inc(parts_done, 1)
                            pool.wait_ge(parts_done, 3 * g + 1)
                            pl.tensor_tensor(p[:, 1, :], f[:, :], zeros[:, :], ALU.add).then_inc(parts_done, 1)
                            pool.wait_ge(parts_done, 3 * g + 2)
                            pl.tensor_tensor(p[:, 2, :], f[:, :], p[:, 1, :], ALU.subtract).then_inc(parts_done, 1)

            walk(pool, phase)
            for n in range(NB):
                pool.wait_ge(fin_stats, n + 1)
                pl.tensor_tensor(rstd[:, n * TB:(n + 1) * TB], rstd[:, n * TB:(n + 1) * TB],
                                 power[:, n * TB:(n + 1) * TB], ALU.pow).then_inc(fin_pow, 1)

        @block.scalar
        def _(act):
            for g in range(TT // 4):
                act.wait_ge(xt_ps, g + 1)
                nc.scalar.copy(srcT[:, g * CH:(g + 1) * CH], half[g]).then_inc(xt_sb, 1)

            def values_a(g):
                act.wait_ge(va_ps, g + 1)
                nc.scalar.copy(vtok_a[:, g * CH:(g + 1) * CH], half[g]).then_inc(va_sb, 1)

            def products(n):
                for w in range(3):
                    act.wait_ge(comp_ps, n + 1)
                    nc.scalar.activation(comp[:, (5 * n + w) * D:(5 * n + w + 1) * D],
                                         half[n % 4][:, w * D:(w + 1) * D], ACT.Copy,
                                         scale=ewb[:, 3 * n + w:3 * n + w + 1]).then_inc(comp_sb, 1)

            act.wait_ge(wb_in, 16 * 11)
            for n in range(2 * NB * NCH):
                act.wait_ge(rope_full, n + 1)
                need(act, a_written[n % STAGES], 3 * 16 * (n // STAGES))
                nc.scalar.copy(parts[n % STAGES][:, 0, :], full[n % STAGES][:, :]).then_inc(rope_hi, 1)
                act.wait_ge(rope_res, n + 1)
                nc.scalar.copy(parts[n % STAGES][:, 1, :], full[n % STAGES][:, :]).then_inc(rope_mid, 1)
                if n == 1:
                    for g in range(TT // 4):
                        values_a(g)
                if n >= 2:
                    products(n - 2)

            def phase(kind, r, c, b):
                ph = PHASES.before(kind, r)
                for k in range(STEPS[kind]):
                    u = UP * ph + k
                    for i in range(TURNS[kind]):
                        which = kind_at(kind, k, 2)
                        if which and i < N_TILES[which]:
                            x0 = PIECES.before(kind, r) + piece_no(kind, k, i)
                            scale = (SCALE_A, SCALE_B)[which == "B"]
                            buf = exps[which][i % N_PROBS[which]]
                            need(act, pv_done, added(kind, r, k - 3) + i - N_PROBS[which] + 1)
                            for n, (lo, hi) in enumerate(pieces(which, i)):
                                bank = (piece_no(kind, k, i) + n) % 2
                                act.wait_ge(s2_ready, x0 + n + 1)
                                nc.scalar.activation(buf[:, lo:hi], s2[bank][:, 0:hi - lo], ACT.Exp,
                                                     scale=scale).then_inc(exp_done, 1)
                        if i == 0 and kind_at(kind, k, 3):
                            act.wait_ge(pv_done, added(kind, r, k - 3))
                            need(act, ctx_out[(k - 3) % 2], 16 * ((UP // 2) * ph + (k - 3) // 2))
                            nc.scalar.copy(csb[(k - 3) % 2][:, :], cps[:, 0:GQ]).then_inc(ctx_sb, 1)
                        if i == MT_SLOT[which_turns(kind)] + 1 and kind_at(kind, k, 1):
                            act.wait_ge(mt_ready, u)
                            need(act, mrow_in[(k - 3) % RING], 16 * (2 * ph + (k - 3) // RING + 1)
                                 if kind_at(kind, k, 3) else 0)
                            nc.scalar.copy(mrows[(k - 1) % 2][:, :], misc_rows).then_inc(mrow_sb, 1)
                        done = (k, i - 1) if i else (k - 1, TURNS[kind] - 1)
                        if done in EXTRA[kind]:
                            extra(kind, r, c, b, ph, *EXTRA[kind][done])

            def extra(kind, r, c, b, ph, what, w):
                preps = PREPS.before(kind, r)
                steps = PREP_STEPS.before(kind, r) + (prep_no(kind, what, w) if what not in ("xa", "fin") else 0)
                if what == "node":
                    act.wait_ge(prep_ps, steps)
                    act.wait_ge(cur_ready, CUR_FIRST + CUR_COPIES.after(kind, r))
                    nc.scalar.activation(srcT[:, bass.ds(c * T + b * S + w * CH, CH)], misc[:, :], ACT.Identity,
                                         bias=cur_bias[:, 2:3]).then_inc(node_ready, 1)
                elif what in ("q", "k"):
                    n = 2 * (what == "k") + w
                    act.wait_ge(prep_ps, steps)
                    act.wait_ge(cur_ready, CUR_FIRST + CUR_COPIES.after(kind, r))
                    need(act, written, 4 * 3 * 16 * preps)
                    bias = cur_bias[:, (what == "k"):(what == "k") + 1]
                    nc.scalar.activation(full[n % STAGES][:, :], misc[:, :], ACT.Identity, bias=bias)
                    nc.scalar.activation(parts[n % STAGES][:, 0, :], misc[:, :], ACT.Identity, bias=bias
                                         ).then_inc(prep_full, 1)
                elif what == "v":
                    act.wait_ge(prep_ps, steps)
                    need(act, vs_ready, UP * ph)
                    nc.scalar.copy(vtok_b[:, bass.ds(b * TB * D + w * CH, CH)], misc[:, :]).then_inc(v_ready, 1)
                elif what == "fin":
                    act.wait_ge(fin_ps, w + 1)
                    nc.scalar.copy(fin[:, w * CH:(w + 1) * CH], misc[:, :]).then_inc(fin_sb, 1)

            walk(act, phase)
            for w in range(2):
                act.wait_ge(fin_ps, 2 + w + 1)
                nc.scalar.copy(fin[:, S + w * CH:S + (w + 1) * CH], misc[:, :]).then_inc(fin_sb, 1)

        @block.vector
        def _(dve):
            ve = nc.vector
            order = [0]

            def after(ins):
                order[0] += 1
                ins.then_inc(dve_order, 1)
                dve.wait_ge(dve_order, order[0])

            def moments(src, t0, tiles):
                for t in range(t0, t0 + tiles):
                    last = ve.bn_stats(stats[:, 6 * t:6 * t + 6], src[:, t * D:(t + 1) * D])
                after(last)
                for t in range(t0, t0 + tiles):
                    last = ve.bn_aggr(mv[:, 2 * t:2 * t + 2], stats[:, 6 * t:6 * t + 6])
                after(last)

            dve.wait_ge(x_in, 16 * NB)
            moments(xtok, 0, TT)
            ve.tensor_scalar_add(rstd[:, :], mv[:, 1:2 * TT:2], EPS_A).then_inc(ln_stats, 1)
            dve.wait_ge(ln_pow, 1)
            for t in range(TT):
                ve.tensor_scalar(xn[:, t * D:(t + 1) * D], xtok[:, t * D:(t + 1) * D], mv[:, 2 * t:2 * t + 1],
                                 rstd[:, t:t + 1], ALU.subtract, ALU.mult).then_inc(xn_ready, 1)

            def rest(n):
                dve.wait_ge(rope_hi, n + 1)
                ve.tensor_tensor(full[n % STAGES][:, :], full[n % STAGES][:, :], parts[n % STAGES][:, 0, :],
                                 ALU.subtract).then_inc(rope_res, 1)

            dve.wait_ge(wa_in, 16 * 7)
            for n in range(2 * NB * NCH):
                w, op = n // 2 % NCH, n % 2
                plain, swapped = ((s2[0], s2[1]), (cps, misc))[n % 2]
                dve.wait_ge(rot_ps, n + 1)
                need(dve, rope_full, n)
                ve.scalar_tensor_tensor(rope[0][:, :], plain[:, :], bias_a[:, 2 * op:2 * op + 1],
                                        table[:, w * CH:(w + 1) * CH], ALU.add, ALU.mult)
                ve.scalar_tensor_tensor(rope[1][:, :], swapped[:, :], bias_a[:, 2 * op + 1:2 * op + 2],
                                        table[:, S + w * CH:S + (w + 1) * CH], ALU.add, ALU.mult
                                        ).then_inc(rot_done, 1)
                dve.wait_ge(rot_done, n + 1)
                need(dve, a_low, n - STAGES + 1)
                ve.tensor_tensor(full[n % STAGES][:, :], rope[0][:, :], rope[1][:, :], ALU.add).then_inc(rope_full, 1)
                if n >= 1:
                    rest(n - 1)
            rest(2 * NB * NCH - 1)

            dve.wait_ge(wb_in, 16 * 11)
            for n in range(NODES):
                ve.tensor_scalar(comp[:, (5 * n + 3) * D:(5 * n + 4) * D], w4_sb[:, (3 * NODES + n) * D:(3 * NODES + n + 1) * D],
                                 actb[:, n:n + 1], None, ALU.mult)
                last = ve.tensor_scalar(comp[:, (5 * n + 4) * D:(5 * n + 5) * D], we_q_sb[:, n * D:(n + 1) * D],
                                        ewb[:, 3 * n:3 * n + 1], None, ALU.mult)
            last.then_inc(wo_ready, 1)
            dve.wait_ge(bias_ps, 1)
            ve.tensor_tensor(vbias[:, :], half[2][:, 0:3 * NODES], ewb[:, :], ALU.mult).then_inc(vbias_ready, 1)
            dve.wait_ge(vbias_ready, 1)
            after(ve.tensor_copy(bias_b[:, :], vbias[:, :]))
            after(ve.tensor_tensor(bias_b[:, 2:3 * NODES:3], be_sb[:, 0:3 * NODES:3], ewb[:, 0:3 * NODES:3], ALU.mult))
            dve.wait_ge(node_bias_ps, 1)
            ve.tensor_tensor(bias_b[:, 2:3 * NODES:3], half[2][:, 32:32 + NODES], bias_b[:, 2:3 * NODES:3],
                             ALU.add).then_inc(bias_done, 1)
            dve.wait_ge(row_ps, 1)
            ve.tensor_tensor(row_o[:, :], half[3][0:1, 0:128], row_o[:, :], ALU.add)
            ve.tensor_copy(row_n[:, :], half[3][0:1, 128:256]).then_inc(row_sb, 1)
            dve.wait_ge(spread_ps, 1)
            after(ve.tensor_tensor(lnb[:, :], half[3][:, 256:384], lnb[:, :], ALU.add))
            xt3 = xtok[:, :].rearrange("p (t d) -> p t d", d=D)
            ve.tensor_tensor(xt3, xt3, lnb[:, :].unsqueeze(1).broadcast_to([128, TT, D]), ALU.add).then_inc(pro_done, 1)
            dve.wait_ge(pro_done, 1)

            def phase(kind, r, c, b):
                ph = PHASES.before(kind, r)
                for k in range(STEPS[kind]):
                    u = UP * ph + k
                    for i in range(TURNS[kind]):
                        if kind != "T":
                            if i == 0:
                                need(dve, max_parts, 4 * (u - 1))
                            n = steps_before(kind, k, 0) + i
                            dve.wait_ge(s1_ready, MAXIMA.before(kind, r) + n + 1)
                            for t, lo, hi in query_tiles(kind[0], i):
                                last = ve.tensor_reduce(neg_max[k % 2][:, t:t + 1], s1[n % 2][:, lo:hi], AX.X,
                                                        ALU.max, negate=True)
                            last.then_inc(max_done, 1)
                        if NORMS.per[kind] and (k, i) == ((2, 7) if kind == "T" else (3, 1)):
                            dve.wait_ge(sums_in, 16 * NORMS.after(kind, r))
                            cols = (HA if kind == "B0" else HB) * S // 128
                            for n in range(NORMS.per[kind]):
                                ve.reciprocal(sums[:, n * cols:(n + 1) * cols], sums[:, n * cols:(n + 1) * cols]
                                              ).then_inc(rec_ready, 1)
                        if EXTRA[kind].get((k, i), ("", 0))[0] == "xa":
                            g = EXTRA[kind][k, i][1]
                            dve.wait_ge(xa_ps, g + 1)
                            ve.tensor_tensor(xtok[:, g * CH:(g + 1) * CH], misc[:, :], xtok[:, g * CH:(g + 1) * CH],
                                             ALU.add).then_inc(xa_done, 1)

            def finish(n):
                dve.wait_ge(fin_sb, NCH * (n + 1))
                moments(fin, n * TB, TB)
                ve.tensor_scalar_add(rstd[:, n * TB:(n + 1) * TB], mv[:, 2 * n * TB + 1:2 * (n + 1) * TB:2], EPS_B
                                     ).then_inc(fin_stats, 1)
                dve.wait_ge(fin_pow, n + 1)
                for t in range(n * TB, (n + 1) * TB):
                    last = ve.tensor_scalar(fin[:, t * D:(t + 1) * D], fin[:, t * D:(t + 1) * D], mv[:, 2 * t:2 * t + 1],
                                            rstd[:, t:t + 1], ALU.subtract, ALU.mult)
                after(last)
                f3 = fin[:, n * S:(n + 1) * S].rearrange("p (t d) -> p t d", d=D)
                after(ve.tensor_tensor(f3, f3, lng[:, :].unsqueeze(1).broadcast_to([128, TB, D]), ALU.mult))
                ve.tensor_tensor(fin[:, n * S:(n + 1) * S], fin[:, n * S:(n + 1) * S], xtok[:, n * S:(n + 1) * S],
                                 ALU.add).then_inc(out_ready, 1)

            walk(dve, phase)
            for n in range(NB):
                finish(n)

        @block.tensor
        def _(pe):
            te = nc.tensor

            def mm(dst, lhsT, rhs, start=True, stop=True):
                return te.matmul(dst, lhsT, rhs, start=start, stop=stop)

            pe.wait_ge(pool_const, 4)
            for t in range(TT):
                pe.wait_ge(xn_ready, t + 1)
                last = te.transpose(half[t // 4][:, t % 4 * 128:(t % 4 + 1) * 128], xn[:, t * D:(t + 1) * D], ident[:, :])
                if t % 4 == 3:
                    last.then_inc(xt_ps, 1)

            def rotate(n):
                chunk, op = n // 2, n % 2
                src = srcT[:, chunk * CH:(chunk + 1) * CH]
                pe.wait_ge(xt_sb, chunk + 1)
                need(pe, rot_done, n - 1)
                for dst, w in zip(((s2[0], s2[1]), (cps, misc))[n % 2], (2 * op, 2 * op + 1)):
                    last = mm(dst[:, :], w_a[:, w * D:(w + 1) * D], src)
                last.then_inc(rot_ps, 1)

            def products(n):
                need(pe, va_sb, min(n + 1, 4))
                need(pe, comp_sb, 3 * (n - 3))
                for w in range(3):
                    last = mm(half[n % 4][:, w * D:(w + 1) * D], we_t_sb[:, (3 * n + w) * D:(3 * n + w + 1) * D],
                              w4_sb[:, (w * NODES + n) * D:(w * NODES + n + 1) * D])
                last.then_inc(comp_ps, 1)

            pe.wait_ge(wa_in, 16 * 7)
            rotate(0)
            rotate(1)
            for g in range(TT // 4):
                pe.wait_ge(xt_sb, g + 1)
                for t in range(4):
                    last = mm(half[g][:, t * D:(t + 1) * D], srcT[:, (4 * g + t) * D:(4 * g + t + 1) * D],
                              w_a[:, 4 * D:5 * D])
                last.then_inc(va_ps, 1)
            pe.wait_ge(wb_in, 16 * 11)
            for n in range(2, 2 * NB * NCH):
                rotate(n)
                products(n - 2)
            pe.wait_ge(comp_sb, 3 * NODES)
            for n in range(NODES):
                for w in range(3):
                    last = mm(half[2][:, 3 * n + w:3 * n + w + 1], w4_sb[:, (w * NODES + n) * D:(w * NODES + n + 1) * D],
                              be_sb[:, 3 * n + w:3 * n + w + 1])
            last.then_inc(bias_ps, 1)
            pe.wait_ge(vbias_ready, 1)
            pe.wait_ge(wo_ready, 1)
            for n in range(NODES):
                last = mm(half[2][:, 32 + n:33 + n], comp[:, (5 * n + 3) * D:(5 * n + 4) * D], vbias[:, 3 * n + 2:3 * n + 3])
            last.then_inc(node_bias_ps, 1)
            pe.wait_ge(bias_done, 1)
            mm(half[3][0:1, 0:128], bias_a[:, 4:5], w_a[:, 5 * D:6 * D])
            mm(half[3][0:1, 128:256], bias_b[:, 3 * NODES - 1:3 * NODES], ident[:, :]).then_inc(row_ps, 1)
            pe.wait_ge(row_sb, 1)
            pe.wait_ge(pool_const, N_CONST)
            mm(half[3][:, 256:384], ones_row[:, :], row_o[:, :]).then_inc(spread_ps, 1)
            pe.wait_ge(pro_done, 1)
            pe.wait_ge(rot_done, 2 * NB * NCH)

            def context(which, u, i, k, exp_no):
                pe.wait_ge(exp_done, exp_no)
                if i == 0:
                    need(pe, ctx_sb, u)
                    pe.wait_ge(vs_ready, u + 1)
                for j, at, q0 in key_tiles(which, i):
                    for g in range(q0 // GQ, S // GQ):
                        lo, hi = max(g * GQ, q0), (g + 1) * GQ
                        last = te.matmul(cps[g * VW:(g + 1) * VW, lo - g * GQ:GQ], vs[k % RING][:, j, :],
                                         exps[which][i % N_PROBS[which]][:, at + lo - q0:at + hi - q0],
                                         start=(i == 0), stop=(j == last_tile(which, g)),
                                         tile_position=(0, g * VW))
                last.then_inc(pv_done, 1)

            def release(kind, r, what, w):
                preps = PREPS.before(kind, r)
                if what == "mt":
                    return mrow_sb, UP * PHASES.before(kind, r) + w
                if what == "node":
                    return node_ready, 2 * NODE_PHASES.before(kind, r) + w + 1
                if what in ("q", "k"):
                    return prep_full, 4 * preps + 2 * (what == "k") + w + 1
                if what == "v":
                    return v_ready, NCH * preps + w + 1
                return (xa_done, w + 1) if what == "xa" else (fin_sb, w + 1)

            def bank_free(kind, r, k, i, extra):
                uses = [(u, MT_SLOT[which_turns(kind)], 0, "mt", u) for u in range(STEPS[kind]) if kind_at(kind, u, 1)]
                uses = sorted(uses + [(*at, 1, *v) for at, v in EXTRA[kind].items()])
                n = [x[:3] for x in uses].index((k, i, int(extra)))
                if n:
                    need(pe, *release(kind, r, *uses[n - 1][3:]))
                else:
                    need(pe, mrow_sb, UP * PHASES.before(kind, r) - 1)

            def extra(kind, r, c, b, what, w):
                cols = slice(w * CH, (w + 1) * CH)
                if what == "node":
                    pe.wait_ge(ctx_ready, NORMS.after(kind, r))
                    pe.wait_ge(cur_ready, CUR_FIRST + CUR_COPIES.after(kind, r))
                    mm(misc[:, :], cur[:, 2 * D:3 * D], ctx_b[:, cols], stop=False)
                    mm(misc[:, :], cur[:, 3 * D:4 * D], srcT[:, bass.ds((c - 1) * T + b * S + w * CH, CH)],
                       start=False).then_inc(prep_ps, 1)
                elif what in ("q", "k"):
                    op = int(what == "k")
                    need(pe, node_ready, 2 * NODE_PHASES.before(kind, r) + (1 if (what, w) == ("q", 0) else 2)
                         if NODE_PHASES.per[kind] else 0)
                    pe.wait_ge(cur_ready, CUR_FIRST + CUR_COPIES.after(kind, r))
                    at = (c // PREV if op else c) * T + b * S + w * CH
                    mm(misc[:, :], cur[:, op * D:(op + 1) * D], srcT[:, bass.ds(at, CH)]).then_inc(prep_ps, 1)
                elif what == "v":
                    pe.wait_ge(vsrc_in, 16 * PREPS.after(kind, r))
                    for t in range(4):
                        last = mm(misc[:, t * D:(t + 1) * D], vsrc[:, w * CH + t * 128:w * CH + (t + 1) * 128],
                                  comp[:, bass.ds(c * 5 * D + 2 * D, D)])
                    last.then_inc(prep_ps, 1)
                elif what == "xa":
                    pe.wait_ge(ctx_ready, NB)
                    for t in range(4):
                        last = mm(misc[:, t * D:(t + 1) * D], ctx_a[:, (4 * w + t) * 128:(4 * w + t + 1) * 128],
                                  w_a[:, 5 * D:6 * D])
                    last.then_inc(xa_ps, 1)
                else:
                    last_node(0, w, NORMS.after(kind, r))

            def last_node(batch, w, norms):
                pe.wait_ge(ctx_ready, norms)
                at = (5 * (NODES - 1)) * D
                for t in range(4 * w, 4 * w + 4):
                    dst, tok = misc[:, t % 4 * D:(t % 4 + 1) * D], slice(t * 128, (t + 1) * 128)
                    src = (NODES - 1) * T + batch * S + t * 128
                    mm(dst, ctx_b[:, tok], comp[:, at + 3 * D:at + 4 * D], stop=False)
                    mm(dst, srcT[:, src:src + 128], comp[:, at + 4 * D:at + 5 * D], start=False, stop=False)
                    last = mm(dst, ones_row[:, :], row_n[:, :], start=False)
                last.then_inc(fin_ps, 1)

            def phase(kind, r, c, b):
                ph = PHASES.before(kind, r)
                for k in range(STEPS[kind]):
                    u = UP * ph + k
                    which = kind_at(kind, k, 2)
                    for i in range(TURNS[kind]):
                        if which and i < N_TILES[which]:
                            q, ky = qs[(k - 2) % RING], ks[(k - 2) % RING]
                            if i == 0:
                                pe.wait_ge(mrow_in[(k - 2) % RING], 16 * (2 * ph + (k - 2) // RING + 1))
                            for n, (lo, hi) in enumerate(pieces(which, i)):
                                x0 = piece_no(kind, k, i) + n
                                bank = s2[x0 % 2]
                                need(pe, exp_done, PIECES.before(kind, r) + x0 - 1)
                                for t, at, q0 in key_tiles(which, i):
                                    first, end = max(lo, at), min(hi, at + S - q0)
                                    if first >= end:
                                        continue
                                    diagonal = which == "A" and first == at
                                    last = mm(bank[:, first - lo:end - lo], ky[0:KALL, t * 128:(t + 1) * 128],
                                              q[0:KALL, q0 + first - at:q0 + end - at], stop=not diagonal)
                                    if diagonal:
                                        last = mm(bank[:, at - lo:at - lo + 128], ident_h[:, :], mask_k[:, :],
                                                  start=False)
                                last.then_inc(s2_ready, 1)
                        if kind != "T":
                            q, ky = qs[k % RING], ks[k % RING]
                            if i == 0:
                                pe.wait_ge(qk_in[k % RING], 32 * (2 * ph + k // RING + 1))
                            n = steps_before(kind, k, 0) + i
                            need(pe, max_done, MAXIMA.before(kind, r) + n - 1)
                            for t, at, end in query_tiles(kind[0], i):
                                for lo, hi in pieces(kind[0], i):
                                    lo, hi = max(lo, at), min(hi, end)
                                    if lo >= hi:
                                        continue
                                    diagonal = kind[0] == "A" and hi == end
                                    last = mm(s1[n % 2][:, lo:hi], q[0:KROW, t * 128:(t + 1) * 128],
                                              ky[0:KROW, lo - at:hi - at], stop=not diagonal)
                                    if diagonal:
                                        last = mm(s1[n % 2][:, end - 128:end], ident_h[:, :], mask_q[:, :],
                                                  start=False)
                            last.then_inc(s1_ready, 1)
                        if i == 0 and kind_at(kind, k, 3):
                            context(kind_at(kind, k, 3), u - 3, N_TILES[kind_at(kind, k, 3)] - 1, k - 3,
                                    PIECES.before(kind, r) + pieces_before(kind, k))
                        elif which and 0 < i < N_TILES[which]:
                            context(which, u - 2, i - 1, k - 2, PIECES.before(kind, r) + piece_no(kind, k, i))
                        if i == MT_SLOT[which_turns(kind)] and kind_at(kind, k, 1):
                            pe.wait_ge(max_parts, 4 * u)
                            bank_free(kind, r, k, i, False)
                            te.transpose(misc_rows, mparts[(k - 1) % 2][:, :], ident_h[:, :]).then_inc(mt_ready, 1)
                        if (k, i) in EXTRA[kind]:
                            bank_free(kind, r, k, i, True)
                            extra(kind, r, c, b, *EXTRA[kind][k, i])

            walk(pe, phase)
            for w in range(NCH):
                pe.wait_ge(fin_sb, NCH + w)
                last_node(1, w, NORMS.after("T", 0))


def rotation_tables():
    import numpy as np

    half = DA // 2
    inv = (1.0 / np.float32(10000.0) ** (np.arange(half, dtype=np.float32) / np.float32(half))).astype(np.float32)
    angles = np.outer(np.arange(S, dtype=np.float32), inv).astype(np.float32)
    cos, sin = np.cos(angles).T, np.sin(angles).T
    cos = np.tile(np.concatenate([cos, cos]), (HA, 1))
    sin = np.tile(np.concatenate([-sin, sin]), (HA, 1))
    return np.ascontiguousarray(cos, dtype=np.float32), np.ascontiguousarray(sin, dtype=np.float32)


def kernel(**inputs):
    import numpy as np
    import concourse.bacc as bacc
    from concourse.bass_utils import run_bass_kernel_spmd as run

    a = {k.replace("L0_", ""): np.asarray(v) for k, v in inputs.items()}
    swap = np.arange(D).reshape(HA, 2, DA // 2)[:, ::-1].reshape(-1)
    w, bias = a["attn_qkv_w"], a["attn_qkv_b"]
    wq_a, wk_a, wv_a = w[0:D], w[D:2 * D], w[2 * D:3 * D]
    bq_a, bk_a, bv_a = bias[0:D], bias[D:2 * D], bias[2 * D:3 * D]
    order = np.array([e for node, _ in edges() for e in node])
    cos, sin = rotation_tables()
    arrays = {
        "x": a["attn_x"].reshape(T, D),
        "w_qk": np.concatenate([wq_a.T, wq_a[swap].T, wk_a.T, wk_a[swap].T], axis=1),
        "w_va": wv_a.T, "w_oa": a["attn_out_w"].T,
        "b_a": np.stack([bq_a, bq_a[swap], bk_a, bk_a[swap], bv_a], axis=1),
        "out_b": a["attn_out_b"].reshape(1, D),
        "cos": cos, "sin": sin,
        "ew": a["ffn_ew"].reshape(1, -1), "act_w": a["ffn_act_w"].reshape(1, -1),
        "we_t": a["ffn_We"][order].transpose(2, 0, 1).reshape(D, -1),
        "we_q": a["ffn_We"][order[0::3]],
        "be": a["ffn_be"][order].T,
        "wq": a["ffn_Wq"], "wk": a["ffn_Wk"], "wv": a["ffn_Wv"], "wo": a["ffn_Wo"],
        "ln_g": a["ffn_ln_g"].reshape(1, D), "ln_b": a["ffn_ln_b"].reshape(1, D),
    }
    arrays = {k: np.ascontiguousarray(v) for k, v in arrays.items()}
    nc = bacc.Bacc("TRN2", target_bir_lowering=False, num_devices=1)
    args = [nc.dram_tensor(f"in_{k}", v.shape, mybir.dt.from_np(v.dtype), kind="ExternalInput").ap()
            for k, v in arrays.items()]
    out = nc.dram_tensor("out", (T, D), F32, kind="ExternalOutput").ap()
    dual_attention_kernel(nc, *args, out)
    r = run(nc, [{f"in_{k}": v for k, v in arrays.items()}], core_ids=[0])
    return r.results[0]["out"].reshape(NB, S, D)
```

```python
import concourse.bass as bass
from concourse import mybir
from contextlib import ExitStack

F32 = mybir.dt.float32
BF16 = mybir.dt.bfloat16
ACT = mybir.ActivationFunctionType
ALU = mybir.AluOpType
AX = mybir.AxisListType

D = 128
NB, S = 2, 1024
T = NB * S
TT = T // 128
TB = S // 128
CH = 512
NCH = S // CH
HA, DA = 16, 8
HB, DB = 8, 16
NODES, PREV = 6, 5
UP = 8
RING = 4
STAGES = 4
KROW = 96
MROW = KROW
KALL = KROW + 3
GQ = 256
VW = 32
LROW = 16
SCALE_A, SCALE_B = DA ** -0.5, DB ** -0.5
EPS_A, EPS_B = 1e-5, 1e-6
MASKED = -1e30
Q_ROWS = [(0, 3, 1), (3, 6, 2), (4, 5, 1)]
K_ROWS = [(2, 5, 1), (1, 6, 4), (0, 1, 1)]


def edges():
    first, out = 0, []
    for c in range(NODES):
        n = min(c + 1, PREV)
        out.append(((first + n - 1, first, first + n // 2), (c, c - n + 1, c - n + 1 + n // 2)))
        first += n
    return out


KEY_TILES = {"A": [[0], [1, 7], [2, 6], [3, 5], [4]], "B": [[j] for j in range(TB)]}
N_TILES = {kind: len(KEY_TILES[kind]) for kind in "AB"}
N_PROBS = {"A": 5, "B": 4}
MT_SLOT = {"A": 1, "B": 3}


def key_tiles(kind, i):
    out, at = [], 0
    for j in KEY_TILES[kind][i]:
        q0 = 128 * j if kind == "A" else 0
        out.append((j, at, q0))
        at += S - q0
    return out


def query_tiles(kind, i):
    if kind == "B":
        return [(i, 0, S)]
    return [(TB - 1 - j, at, at + S - q0) for j, at, q0 in key_tiles(kind, i)]


def width(kind, i):
    return query_tiles(kind, i)[-1][2]


def pieces(kind, i):
    return [(lo, min(lo + CH, width(kind, i))) for lo in range(0, width(kind, i), CH)]


def last_tile(kind, g):
    return [j for tiles in KEY_TILES[kind] for j in tiles if kind == "B" or 128 * j < GQ * (g + 1)][-1]


N_PIECES = {k: sum(len(pieces(k, j)) for j in range(N_TILES[k])) for k in "AB"}
NODE_AT = {(4, 1): ("node", 0), (4, 5): ("node", 1)}
PREP_AT = {(4, 7): ("q", 0), (5, 1): ("q", 1), (5, 5): ("k", 0), (5, 7): ("k", 1),
           (6, 1): ("v", 0), (6, 5): ("v", 1)}
PREP_A_AT = {(2, 2): ("q", 0), (3, 2): ("q", 1), (4, 2): ("k", 0), (5, 2): ("k", 1),
             (6, 2): ("v", 0), (6, 4): ("v", 1)}
XA_AT = {(1, 1): ("xa", 0), (1, 5): ("xa", 1), (2, 1): ("xa", 2), (2, 5): ("xa", 3)}
FIN_AT = {(4, 1): ("fin", 0), (4, 5): ("fin", 1)}

START_AT = {(0, 0): ("bias", 1), (0, 1): ("bias", 2), (0, 2): ("bias", 3),
            (0, 4): ("rot", 8), (1, 2): ("rot", 9), (1, 4): ("rot", 10), (2, 2): ("rot", 11),
            (2, 4): ("rot", 12), (3, 2): ("rot", 13), (3, 4): ("rot", 14), (4, 2): ("rot", 15),
            (4, 4): ("va", 2), (5, 2): ("va", 3)}

KINDS = ["A0", "AL", "AZ", "B0", "BL", "BE", "T"]
TIMES = {"A0": 1, "AL": NB * HA // UP - 2, "AZ": 1, "B0": 1, "BL": (NODES - 1) * NB, "BE": 1, "T": 1}
EXTRA = {"A0": START_AT, "AL": {}, "AZ": PREP_A_AT, "B0": PREP_AT, "BL": {**NODE_AT, **PREP_AT},
         "BE": {**XA_AT, **FIN_AT}, "T": {}}
PREPARES = ("AZ", "B0", "BL")
CUT_AT = {**{k: {} for k in ("A0", "AL", "BE", "T")}, "AZ": {3: [0], 4: [1], 5: [2], 6: [3]},
          "B0": {5: [0, 1], 6: [2, 3]}, "BL": {5: [0, 1], 6: [2, 3]}}
READ_AT = {"B0": {2: [0], 3: [1]}, "BL": {2: [0]}, "BE": {2: [0]}, "T": {2: [0]}}
SPREAD_AT = {"B0": 4, "BL": 3, "BE": 3, "T": 2}
NORM_AT = {"B0": 7, "BL": 3, "BE": 3}
STEPS = {k: 3 if k == "T" else UP for k in KINDS}
TURNS = {k: N_TILES["A"] if k[0] == "A" else TB for k in KINDS}


def step_at(kind, which, turn):
    if which is None:
        return None
    turns = [0, 2, 3, 5, 6] if which == "A" and kind[0] != "A" else list(range(N_TILES[which]))
    return turns.index(turn) if turn in turns else None


def which_turns(kind):
    return "A" if kind[0] == "A" else "B"


def kind_at(kind, k, lag):
    if k - lag >= 0:
        return None if kind == "T" else kind[0]
    return {"A0": None, "AL": "A", "AZ": "A", "B0": "A", "BL": "B", "BE": "B", "T": "B"}[kind]


class Count:

    def __init__(self, **per):
        self.per = {k: per.get(k, 0) for k in KINDS}

    def before(self, kind, r):
        n = sum(self.per[x] * TIMES[x] for x in KINDS[:KINDS.index(kind)])
        return n + r * self.per[kind] if TIMES[kind] > 1 and self.per[kind] else n

    def after(self, kind, r):
        return self.before(kind, r) + self.per[kind]


def pieces_before(kind, k):
    return sum(N_PIECES[kind_at(kind, u, 2)] for u in range(k) if kind_at(kind, u, 2))


def steps_before(kind, k, lag):
    return sum(N_TILES[kind_at(kind, u, lag)] for u in range(k) if kind_at(kind, u, lag))


PHASES = Count(A0=1, AL=1, AZ=1, B0=1, BL=1, BE=1)
PIECES = Count(**{k: pieces_before(k, STEPS[k]) for k in KINDS})
MAXIMA = Count(**{k: steps_before(k, UP, 0) for k in KINDS if k != "T"})
ADDED = Count(**{k: steps_before(k, STEPS[k], 2) for k in KINDS})
PREPS = Count(AZ=1, B0=1, BL=1)
PREP_STEPS = Count(**{k: len(EXTRA[k]) for k in ("AZ", "B0", "BL")})
NODE_PHASES = Count(BL=1)
NORMS = Count(B0=NB, BL=1, BE=1, T=1)
CUR_COPIES = Count(BL=4)
CUR_FIRST = 2
FINISH = [(0, TB), (TB, TB // 2), (TB + TB // 2, TB // 2)]
N_CONST = 10 + 2 * RING


def added(kind, r, k):
    if k < -3:
        return ADDED.before(kind, r) - (N_TILES[kind_at(kind, 0, 3)] if kind_at(kind, 0, 3) else 0)
    return ADDED.before(kind, r) + steps_before(kind, k + 3, 2)


def piece_no(kind, k, j):
    which = kind_at(kind, k, 2)
    return pieces_before(kind, k) + sum(len(pieces(which, t)) for t in range(j))


def prep_no(kind, what, w):
    return [v for _, v in sorted(EXTRA[kind].items())].index((what, w)) + 1


def dual_attention_kernel(nc, x, w_qk, w_va, w_oa, b_a, out_b, cos, sin, ew, act_w, we_t, we_q,
                          be, wq, wk, wv, wo, ln_g, ln_b, out):
    ctx = ExitStack()
    with ctx:
        def sb(name, shape, dt=F32):
            return ctx.enter_context(nc.sbuf_tensor(name, shape, dt))

        def pb(name, shape, dt=F32):
            return ctx.enter_context(nc.psum_tensor(name, shape, dt))

        def sem(name):
            return ctx.enter_context(nc.semaphore(name))

        qk_dram = {"A": nc.dram_tensor("dram_qk_a", (2, 6, NB * HA * DA, S), BF16).ap(),
                   "B": nc.dram_tensor("dram_qk_b", (2, 6, NB * HB * DB, S), BF16).ap()}
        raw_dram = {"A": nc.dram_tensor("dram_raw_a", (NB * HA, 128, GQ), F32).ap(),
                    "B": nc.dram_tensor("dram_raw_b", (NB * HB, 128, GQ), F32).ap()}
        rec_dram = {"A": nc.dram_tensor("dram_rec_a", (NB, HA, S), F32).ap(),
                    "B": nc.dram_tensor("dram_rec_b", (NB, HB, S), F32).ap()}

        srcT = sb("srcT", [128, NODES * T])
        xtok = sb("xtok", [128, TT * D])
        qs = [sb(f"qs{s}", [128, S], BF16) for s in range(RING)]
        ks = [sb(f"ks{s}", [128, S], BF16) for s in range(RING)]
        vs = [sb(f"vs{s}", [128, TB, VW]) for s in range(RING)]
        probs = [sb(f"probs{s}", [128, S]) for s in range(N_PROBS["B"])]
        vtok_a = sb("vtok_a", [128, TT * D])
        vtok_b = sb("vtok_b", [128, NB * TB * D])
        comp = sb("comp", [128, NODES * 5 * D])
        cur = sb("cur", [128, 4 * D])
        cur_bias = sb("cur_bias", [128, 3])
        bias_b = sb("bias_b", [128, NODES * 3])
        w_a = sb("w_a", [128, 6 * D])
        bias_a = sb("bias_a", [128, 5])
        ctx_a = sb("ctx_a", [128, T])
        table = sb("table", [128, 2 * S])
        ctx_b = sb("ctx_b", [128, S])
        rec_b = sb("rec_b", [128, S])
        vsrc = sb("vsrc", [128, S])
        full = [sb(f"full{s}", [128, CH]) for s in range(STAGES)]
        parts = [sb(f"parts{s}", [128, 3, CH], BF16) for s in range(STAGES)]
        csb = [sb(f"csb{s}", [128, GQ]) for s in range(2)]
        neg_max = [sb(f"neg_max{s}", [128, TB]) for s in range(2)]
        mres = sb("mres", [128, TB])
        mparts = [sb(f"mparts{s}", [128, 3 * TB], BF16) for s in range(2)]
        mrows = [sb(f"mrows{s}", [3 * TB, 128], BF16) for s in range(2)]
        sums = sb("sums", [128, 4 * 64])
        rope = [sb(f"rope{s}", [128, CH]) for s in range(2)]
        ident = sb("ident", [128, 128])
        ident_h = sb("ident_h", [128, 128], BF16)
        mask_q = sb("mask_q", [128, 128], BF16)
        mask_k = sb("mask_k", [128, 128], BF16)
        ones_row = sb("ones_row", [1, 128])
        ewb = sb("ewb", [128, NODES * 3])
        actb = sb("actb", [128, NODES])
        be_sb = sb("be_sb", [128, NODES * 3])
        vbias = sb("vbias", [128, NODES * 3])
        row_o = sb("row_o", [1, 128])
        row_n = sb("row_n", [1, 128])
        lng = sb("lng", [128, D])
        lnb = sb("lnb", [128, D])
        stats = sb("stats", [128, TT * 6])
        mv = sb("mv", [128, TT * 2])
        rstd = sb("rstd", [128, TT])
        power = sb("power", [128, TT])
        zeros = sb("zeros", [128, CH])
        fin = sb("fin", [128, T])

        raw_w = srcT[:, 2 * T:5 * T]
        we_t_sb = raw_w[:, 0:NODES * 3 * D]
        we_q_sb = raw_w[:, NODES * 3 * D:NODES * 4 * D]
        w4_sb = raw_w[:, NODES * 4 * D:NODES * 8 * D]
        xn = fin
        exps = {"B": probs, "A": probs + [rec_b]}

        s1 = [pb(f"s1_{n}", [128, S]) for n in range(2)]
        s2 = [pb(f"s2_{n}", [128, CH]) for n in range(2)]
        cps = pb("cps", [128, CH])
        misc = pb("misc", [128, CH])

        sems = ("wqk_in wa_in wb_in dve_const pool_const ln_stats ln_pow xn_ready xt_ps xt_sb dve_order rot_ps rot_done "
                "rope_full rope_hi rope_res rope_mid a_low va_ps va_sb comp_ps comp_sb wo_ready bias_ps bias_used x_ready "
                "cur_ready s1_ready max_done max_parts "
                "mt_ready mrow_sb s2_ready exp_done pv_done ctx_sb vs_ready prep_ps prep_full parts_done v_ready "
                "node_ready vsrc_in sums_in ctx_in rec_ready rec_out rec_in ctx_ready last_ctx xa_ps xa_done fin_ps fin_sb "
                "fin_stats fin_pow out_ready stored")
        (wqk_in, wa_in, wb_in, dve_const, pool_const, ln_stats, ln_pow, xn_ready, xt_ps, xt_sb, dve_order, rot_ps, rot_done,
         rope_full, rope_hi, rope_res, rope_mid, a_low, va_ps, va_sb, comp_ps, comp_sb, wo_ready, bias_ps,
         bias_used, x_ready, cur_ready, s1_ready, max_done,
         max_parts, mt_ready, mrow_sb, s2_ready, exp_done, pv_done, ctx_sb, vs_ready, prep_ps, prep_full,
         parts_done, v_ready, node_ready, vsrc_in, sums_in, ctx_in, rec_ready, rec_out, rec_in, ctx_ready, last_ctx, xa_ps,
         xa_done, fin_ps, fin_sb, fin_stats, fin_pow, out_ready, stored) = [sem(n) for n in sems.split()]
        x_in = [sem(f"x_in{n}") for n in range(NB)]
        qk_in = [sem(f"qk_in{n}") for n in range(RING)]
        mrow_in = [sem(f"mrow_in{n}") for n in range(RING)]
        ctx_out = [sem(f"ctx_out{n}") for n in range(2)]
        written = sem("written")
        a_written = [sem(f"a_written{n}") for n in range(STAGES)]
        half = [s1[n // 2][:, n % 2 * CH:(n % 2 + 1) * CH] for n in range(4)]
        misc_rows = misc[0:3 * TB, 0:64].bitcast(BF16)

        def need(eng, s, value):
            if isinstance(value, int) and value <= 0:
                return
            eng.wait_ge(s, value)

        def walk(eng, phase):
            phase("A0", 0, 0, 0)
            with eng.Fori(0, TIMES["AL"]) as r:
                phase("AL", r, 0, 0)
            phase("AZ", 0, 0, 0)
            phase("B0", 0, 0, 1)
            with eng.Fori(1, NODES) as c:
                with eng.Fori(0, NB) as b:
                    phase("BL", (c - 1) * NB + b, c, b)
            phase("BE", 0, 0, 0)
            phase("T", 0, 0, 1)

        def head_row(kind, r, k, b):
            if kind[0] == "A" or kind == "B0" and k < 0:
                return {"A0": 0, "AL": r * UP + UP, "AZ": 3 * UP, "B0": 4 * UP}[kind] + k
            here = {"B0": 0, "BL": b * -1 + 1, "BE": 1, "T": 0}[kind]
            other = {"B0": 1, "BL": b, "BE": 0, "T": 1}[kind]
            return here * HB + k if 0 <= k < UP else other * HB + k % UP

        block = ctx.enter_context(nc.Block())

        @block.sync
        def _(sp):
            xt = x.rearrange("(t p) d -> p t d", p=128)

            def load_x(h):
                sp.dma_start(xtok[:, h * S:(h + 1) * S].rearrange("p (t d) -> p t d", d=D),
                             xt[:, h * TB:(h + 1) * TB, :]).then_inc(x_in[h], 16)

            load_x(0)
            sp.dma_start(w_a[:, 0:4 * D], w_qk).then_inc(wqk_in, 16)
            load_x(1)
            sp.dma_start(bias_a[:, :], b_a).then_inc(wa_in, 16)
            sp.dma_start(table[:, 0:S], cos).then_inc(wa_in, 16)
            sp.dma_start(table[:, S:2 * S], sin).then_inc(wa_in, 16)
            sp.dma_start(w_a[:, 4 * D:5 * D], w_va).then_inc(wa_in, 16)
            sp.dma_start(w_a[:, 5 * D:6 * D], w_oa).then_inc(wa_in, 16)
            sp.dma_start(row_o[:, :], out_b).then_inc(wa_in, 16)
            sp.dma_start(ewb[:, :], ew.partition_broadcast(128)).then_inc(wb_in, 16)
            sp.dma_start(actb[:, :], act_w.partition_broadcast(128)).then_inc(wb_in, 16)
            sp.dma_start(be_sb[:, :], be).then_inc(wb_in, 16)
            sp.dma_start(we_t_sb, we_t).then_inc(wb_in, 16)
            sp.dma_start(we_q_sb.rearrange("p (n d) -> p n d", n=NODES),
                         we_q.rearrange("n p d -> p n d")).then_inc(wb_in, 16)
            for n, w in enumerate((wq, wk, wv, wo)):
                sp.dma_start(w4_sb[:, n * NODES * D:(n + 1) * NODES * D].rearrange("p (n d) -> p n d", n=NODES),
                             w.rearrange("n p d -> p n d")).then_inc(wb_in, 16)
            sp.dma_start(lng[:, :], ln_g.partition_broadcast(128)).then_inc(wb_in, 16)
            sp.dma_start(lnb[:, :], ln_b.partition_broadcast(128)).then_inc(wb_in, 16)

            def write_parts(which, n, rows, op, w, done, parts_ready, only=(0, 1, 2)):
                for part in only:
                    lo, hi, step = (Q_ROWS, K_ROWS)[op][part]
                    groups = len(range(lo, hi, step))
                    sp.wait_ge(*parts_ready[part])
                    sp.dma_start(qk_dram[which][op, lo:hi:step, rows, w * CH:(w + 1) * CH
                                                ].rearrange("r p s -> p r s"),
                                 parts[n % STAGES][:, part:part + 1, :].broadcast_to([128, groups, CH])
                                 ).then_inc(done, 16)

            def write_a(n, only=(0, 1, 2)):
                b, w, op = n // (2 * NCH), n // 2 % NCH, n % 2
                write_parts("A", n, slice(b * 128, (b + 1) * 128), op, w, a_written[n % STAGES],
                            [(rope_hi, n + 1), (rope_mid, n + 1), (a_low, n + 1)], only)

            for n in range(2 * NCH):
                write_a(n, [0])
                if n:
                    write_a(n - 1, [2])
                write_a(n, [1])
            write_a(2 * NCH - 1, [2])
            for s in a_written:
                sp.wait_ge(s, 3 * 16)

            def load_unit(kind, r, k, b):
                which = "B" if kind[0] == "B" or (kind, k) == ("AZ", UP) else "A"
                row = 0 if (kind, k) == ("AZ", UP) else head_row(kind, r, k, b)
                dims, slot = (DA, DB)[which == "B"], k % RING
                if k < UP:
                    need(sp, pv_done, added(kind, r, k - RING))
                else:
                    need(sp, written, 4 * 3 * 16 * PREPS.after(kind, r))
                for op, dst in ((0, qs[slot]), (1, ks[slot])):
                    sp.dma_start(dst[0:6 * dims, :],
                                 qk_dram[which][op, :, bass.ds(row * dims, dims), :]
                                 ).then_inc(qk_in[slot], 16)

            sp.wait_ge(dve_const, 3 * RING)
            sp.wait_ge(pool_const, N_CONST)
            load_unit("A0", 0, 0, 0)

            def store(n):
                t0, tiles = FINISH[n]
                sp.wait_ge(out_ready, n + 1)
                sp.dma_start(out.rearrange("(t p) d -> p t d", p=128)[:, t0:t0 + tiles, :],
                             fin[:, t0 * D:(t0 + tiles) * D].rearrange("p (t d) -> p t d", d=D)).then_inc(stored, 16)

            def norm_batches(kind, b):
                return {"B0": [0, 1], "BL": [b], "BE": [0], "T": [1]}.get(kind, [])

            def read_before(kind, r, b, which_of, what):
                which, heads, width = ("A", HA, DA) if kind == "B0" else ("B", HB, DB)
                cols = heads * S // 128
                for n in which_of:
                    batch = norm_batches(kind, b)[n]
                    raw = raw_dram[which][bass.ds(batch * heads, heads), :, :]
                    if what == "sums":
                        sp.dma_start(sums[:, n * cols:(n + 1) * cols],
                                     raw[:, LROW:128:VW, :].rearrange("h g (a n) -> h g a n", n=cols)
                                     ).then_inc(sums_in, 16)
                        continue
                    dst = ctx_a[:, n * S:(n + 1) * S] if which == "A" else ctx_b
                    for g in range(S // GQ):
                        sp.dma_start(dst[:, g * GQ:(g + 1) * GQ], raw[:, g * VW:g * VW + width, :]
                                     ).then_inc(ctx_in, 16)

            def spread_reciprocals(kind, r, b):
                which, heads, width = ("A", HA, DA) if kind == "B0" else ("B", HB, DB)
                cols = heads * S // 128
                sp.wait_ge(rec_ready, NORMS.after(kind, r))
                for n, batch in enumerate(norm_batches(kind, b)):
                    sp.dma_start(rec_dram[which][bass.ds(batch, 1), :, :].rearrange("o h (a n) -> (o h a) n", n=cols),
                                 sums[:, n * cols:(n + 1) * cols]).then_inc(rec_out, 16)
                sp.wait_ge(rec_out, 16 * NORMS.after(kind, r))
                for n, batch in enumerate(norm_batches(kind, b)):
                    dst = table[:, n * S:(n + 1) * S] if which == "A" else rec_b[:, :]
                    src = rec_dram[which][bass.ds(batch, 1), :, :].rearrange("o h n -> (o h) n")
                    sp.dma_start(dst, src.unsqueeze(1).broadcast_to([heads, width, S])).then_inc(rec_in, 16)

            def phase(kind, r, c, b):
                ph = PHASES.before(kind, r)
                for k in range(STEPS[kind]):
                    u = UP * ph + k
                    if k < UP - 1 and kind != "T":
                        load_unit(kind, r, k + 1, b)
                    if kind_at(kind, k, 3):
                        sp.wait_ge(ctx_sb, u - 2)
                        sp.dma_start(raw_dram[kind_at(kind, k, 3)][bass.ds(head_row(kind, r, k - 3, b), 1), :, :
                                                                   ].rearrange("o p n -> (o p) n"),
                                     csb[(k - 3) % 2][:, :]).then_inc(ctx_out[(k - 3) % 2], 16)
                    if k in READ_AT.get(kind, {}):
                        for s in ctx_out if k == 2 else ():
                            sp.wait_ge(s, 16 * (UP // 2) * ph)
                        sp.wait_ge(prep_ps, PREP_STEPS.before(kind, r))
                        if kind == "T":
                            sp.wait_ge(fin_ps, 2)
                        read_before(kind, r, b, READ_AT[kind][k], "sums")
                    if k == SPREAD_AT.get(kind):
                        spread_reciprocals(kind, r, b)
                    if kind_at(kind, k, 1):
                        sp.wait_ge(mrow_sb, u)
                        sp.dma_start(qs[(k - 1) % RING][MROW:KALL, :].rearrange("a (i n) -> a i n", n=128),
                                     mrows[(k - 1) % 2][:, :]).then_inc(mrow_in[(k - 1) % RING], 16)
                    if k in READ_AT.get(kind, {}):
                        read_before(kind, r, b, READ_AT[kind][k], "contexts")
                    if kind == "A0" and 3 <= k < 3 + 2 * NCH:
                        write_a(2 * NCH + k - 3)
                    if kind == "A0" and k == UP - 1:
                        for s in a_written:
                            sp.wait_ge(s, 2 * 3 * 16)
                    if kind in PREPARES and k == 5:
                        need(sp, node_ready, 2 * NODE_PHASES.after(kind, r))
                        need(sp, prep_ps, PREP_STEPS.before(kind, r))
                        sp.dma_start(vsrc[:, :], srcT[:, bass.ds((c + 1) // 2 * T + b * S, S)]
                                     ).then_inc(vsrc_in, 16)
                    for n in CUT_AT[kind].get(k, []):
                        g = 4 * PREPS.before(kind, r) + n
                        write_parts("B", n, bass.ds(b * 128, 128), n // 2, n % 2, written,
                                    [(parts_done, 4 * g + 1), (parts_done, 4 * g + 3), (parts_done, 4 * g + 4)])
                    if k == UP - 1 and kind not in ("BE", "T"):
                        load_unit(kind, r, UP, b)
                    if kind == "T" and k == 1:
                        store(0)

            walk(sp, phase)
            for n in range(1, len(FINISH)):
                store(n)
            sp.wait_ge(stored, 16 * len(FINISH))
            for s in ctx_out:
                sp.wait_ge(s, 16 * UP // 2 * (NB * HA // UP + NODES * NB))
            sp.wait_ge(written, 4 * 3 * 16 * NODES * NB)
            sp.wait_ge(rec_out, 16 * NORMS.after("T", 0))

        @block.gpsimd
        def _(pool):
            pl = nc.gpsimd
            pl.memset(ident[:, :], 0.0).then_inc(pool_const, 1)
            pl.memset(mask_q[:, :], 0.0).then_inc(pool_const, 1)
            pl.memset(mask_k[:, :], 0.0).then_inc(pool_const, 1)
            pool.wait_ge(pool_const, 3)
            pl.affine_select(out=ident[:, :], in_=ident[:, :], pattern=[[-1, 128]], compare_op=ALU.not_equal,
                             fill=1.0, base=0, channel_multiplier=1).then_inc(pool_const, 1)
            pl.memset(power[:, :], -0.5).then_inc(pool_const, 1)
            pool.wait_ge(pool_const, 5)
            pl.tensor_copy(ident_h[:, :], ident[:, :]).then_inc(pool_const, 1)
            for n in range(NB):
                pool.wait_ge(ln_stats, n + 1)
                pl.tensor_tensor(rstd[:, n * TB:(n + 1) * TB], rstd[:, n * TB:(n + 1) * TB],
                                 power[:, n * TB:(n + 1) * TB], ALU.pow).then_inc(ln_pow, 1)
            pl.affine_select(out=mask_q[:, :], in_=mask_q[:, :], pattern=[[-1, 128]], compare_op=ALU.is_ge,
                             fill=MASKED, base=0, channel_multiplier=1).then_inc(pool_const, 1)
            pl.affine_select(out=mask_k[:, :], in_=mask_k[:, :], pattern=[[1, 128]], compare_op=ALU.is_ge,
                             fill=MASKED, base=0, channel_multiplier=-1).then_inc(pool_const, 1)
            pl.memset(ones_row[:, :], 1.0).then_inc(pool_const, 1)
            pl.memset(zeros[:, :], 0.0).then_inc(pool_const, 1)
            pool.wait_ge(dve_const, 3 * RING)
            for s in range(RING):
                pl.memset(vs[s][:, :, LROW:LROW + 1], 1.0).then_inc(pool_const, 1)
            for s in range(RING):
                pool.wait_ge(pool_const, N_CONST - RING + s)
                pl.memset(ks[s][MROW:128, :], 1.0).then_inc(pool_const, 1)
            pool.wait_ge(pool_const, N_CONST)
            def low_part(n):
                pool.wait_ge(rope_mid, n + 1)
                pl.tensor_tensor(parts[n % STAGES][:, 2, :], full[n % STAGES][:, :], parts[n % STAGES][:, 1, :],
                                 ALU.subtract).then_inc(a_low, 1)

            def deviations(n):
                t0, tiles = FINISH[n]
                pool.wait_ge(fin_stats, n + 1)
                pl.tensor_tensor(rstd[:, t0:t0 + tiles], rstd[:, t0:t0 + tiles], power[:, t0:t0 + tiles], ALU.pow
                                 ).then_inc(fin_pow, 1)

            def rest(n):
                pool.wait_ge(rope_hi, n + 1)
                pl.tensor_tensor(full[n % STAGES][:, :], full[n % STAGES][:, :], parts[n % STAGES][:, 0, :],
                                 ALU.subtract).then_inc(rope_res, 1)

            rest(0)
            for n in range(1, 2 * NCH):
                if n < 2 * NCH - 1:
                    rest(n)
                low_part(n - 1)
            low_part(2 * NCH - 1)

            def phase(kind, r, c, b):
                ph = PHASES.before(kind, r)
                for k in range(STEPS[kind]):
                    u = UP * ph + k
                    if kind_at(kind, k, 1):
                        v, nm, mp = u - 1, neg_max[(k - 1) % 2], mparts[(k - 1) % 2]
                        pool.wait_ge(max_done, MAXIMA.before(kind, r) + (steps_before(kind, k, 0) if k else 0))
                        need(pool, mt_ready, v - 1)
                        pl.tensor_tensor(mp[:, 0:TB], nm[:, :], zeros[:, 0:TB], ALU.add).then_inc(max_parts, 1)
                        pool.wait_ge(max_parts, 4 * v + 1)
                        pl.tensor_tensor(mres[:, :], nm[:, :], mp[:, 0:TB], ALU.subtract).then_inc(max_parts, 1)
                        pool.wait_ge(max_parts, 4 * v + 2)
                        pl.tensor_tensor(mp[:, TB:2 * TB], mres[:, :], zeros[:, 0:TB], ALU.add).then_inc(max_parts, 1)
                        pool.wait_ge(max_parts, 4 * v + 3)
                        pl.tensor_tensor(mp[:, 2 * TB:3 * TB], mres[:, :], mp[:, TB:2 * TB],
                                         ALU.subtract).then_inc(max_parts, 1)
                    if kind != "T":
                        which = kind[0]
                        dims = (DA, DB)[which == "B"]
                        batch = {"A0": 0, "AL": r, "AZ": 1, "B0": 0, "BL": b * -1 + 1, "BE": 1}[kind]
                        head = {"AL": (r * -1 + 1) * UP, "AZ": UP}.get(kind, 0) + k
                        need(pool, pv_done, added(kind, r, k - RING))
                        if kind in ("A0", "AL") and k == 0:
                            pool.wait_ge(va_sb, TT // 4 if kind == "AL" else TB // 4)
                        if which == "B":
                            pool.wait_ge(v_ready, NCH * PREPS.before(kind, r))
                        src = (vtok_a, vtok_b)[which == "B"][:, :].rearrange("p (t d) -> p t d", d=D)
                        pl.tensor_copy(vs[k % RING][:, :, 0:dims],
                                       src[:, bass.ds(batch * TB, TB), bass.ds(head * dims, dims)]
                                       ).then_inc(vs_ready, 1)
                    if kind == "A0" and k == 0:
                        pool.wait_ge(bias_used, 4)
                        xt3 = xtok[:, :].rearrange("p (t d) -> p t d", d=D)
                        pl.tensor_tensor(xt3, xt3, lnb[:, :].unsqueeze(1).broadcast_to([128, TT, D]), ALU.add
                                         ).then_inc(x_ready, 1)
                    if kind == "A0" and 2 <= k < 2 + 2 * NCH:
                        n = 2 * NCH + k - 2
                        rest(n)
                        low_part(n)
                    if kind == "A0" and k == UP - 1:
                        pool.wait_ge(comp_sb, 3 * NODES)
                        pool.wait_ge(bias_used, 2)
                        pl.tensor_copy(cur[:, 0:2 * D], comp[:, 0:2 * D]).then_inc(cur_ready, 1)
                        pl.tensor_copy(cur_bias[:, 0:2], bias_b[:, 0:2]).then_inc(cur_ready, 1)
                    if kind == "BL" and k == 0:
                        pool.wait_ge(mrow_sb, u - 1)
                        pl.tensor_tensor(cur[:, 0:2 * D], comp[:, bass.ds(c * 5 * D, 2 * D)], zeros[:, 0:2 * D],
                                         ALU.add).then_inc(cur_ready, 1)
                        pl.tensor_copy(cur[:, 2 * D:4 * D], comp[:, bass.ds(c * 5 * D - 2 * D, 2 * D)]
                                       ).then_inc(cur_ready, 1)
                        pl.tensor_copy(cur_bias[:, 0:2], bias_b[:, bass.ds(c * 3, 2)]).then_inc(cur_ready, 1)
                        pl.tensor_copy(cur_bias[:, 2:3], bias_b[:, bass.ds(c * 3 - 1, 1)]).then_inc(cur_ready, 1)
                    if kind == "T" and k == 0:
                        deviations(0)
                    if k == NORM_AT.get(kind):
                        pool.wait_ge(rec_in, 16 * NORMS.after(kind, r))
                        pool.wait_ge(ctx_in, 16 * (S // GQ) * NORMS.after(kind, r))
                        if kind == "B0":
                            for n in range(NB):
                                pl.tensor_tensor(ctx_a[:, n * S:(n + 1) * S], ctx_a[:, n * S:(n + 1) * S],
                                                 table[:, n * S:(n + 1) * S], ALU.mult).then_inc(ctx_ready, 1)
                        else:
                            pl.tensor_tensor(ctx_b[:, :], ctx_b[:, :], rec_b[:, :], ALU.mult).then_inc(ctx_ready, 1)
                    for n in CUT_AT[kind].get(k, []):
                        g = 4 * PREPS.before(kind, r) + n
                        f, p = full[n % STAGES], parts[n % STAGES]
                        pool.wait_ge(prep_full, g + 1)
                        pl.tensor_tensor(p[:, 0, :], f[:, :], zeros[:, :], ALU.add).then_inc(parts_done, 1)
                        pool.wait_ge(parts_done, 4 * g + 1)
                        pl.tensor_tensor(f[:, :], f[:, :], p[:, 0, :], ALU.subtract).then_inc(parts_done, 1)
                        pool.wait_ge(parts_done, 4 * g + 2)
                        pl.tensor_tensor(p[:, 1, :], f[:, :], zeros[:, :], ALU.add).then_inc(parts_done, 1)
                        pool.wait_ge(parts_done, 4 * g + 3)
                        pl.tensor_tensor(p[:, 2, :], f[:, :], p[:, 1, :], ALU.subtract).then_inc(parts_done, 1)

            walk(pool, phase)
            for n in range(1, len(FINISH)):
                deviations(n)

        @block.scalar
        def _(act):
            def transposed(g):
                act.wait_ge(xt_ps, g + 1)
                nc.scalar.copy(srcT[:, g * CH:(g + 1) * CH], half[g]).then_inc(xt_sb, 1)

            def high_part(n):
                act.wait_ge(rope_full, n + 1)
                need(act, a_written[n % STAGES], 3 * 16 * (n // STAGES))
                nc.scalar.copy(parts[n % STAGES][:, 0, :], full[n % STAGES][:, :]).then_inc(rope_hi, 1)

            def middle_part(n):
                act.wait_ge(rope_res, n + 1)
                nc.scalar.copy(parts[n % STAGES][:, 1, :], full[n % STAGES][:, :]).then_inc(rope_mid, 1)

            def values_a(g):
                act.wait_ge(va_ps, g + 1)
                nc.scalar.copy(vtok_a[:, g * CH:(g + 1) * CH], half[2 + g]).then_inc(va_sb, 1)

            def products(n):
                for w in range(3):
                    act.wait_ge(comp_ps, n + 1)
                    nc.scalar.activation(comp[:, (5 * n + w) * D:(5 * n + w + 1) * D],
                                         half[n % 4][:, w * D:(w + 1) * D], ACT.Copy,
                                         scale=ewb[:, 3 * n + w:3 * n + w + 1]).then_inc(comp_sb, 1)

            transposed(0)
            transposed(1)
            for n in range(2 * NCH):
                high_part(n)
                if n == 0:
                    transposed(2)
                    transposed(3)
                middle_part(n)
            act.wait_ge(wb_in, 16 * 11)
            products(0)
            products(1)
            for g in range(TB // 4):
                values_a(g)
            for n in range(2, NODES):
                products(n)

            def phase(kind, r, c, b):
                ph = PHASES.before(kind, r)
                for k in range(STEPS[kind]):
                    u = UP * ph + k
                    for i in range(TURNS[kind]):
                        if i == MT_SLOT[which_turns(kind)] + 1 and kind_at(kind, k, 1):
                            act.wait_ge(mt_ready, u)
                            need(act, mrow_in[(k - 3) % RING], 16 * (2 * ph + (k - 3) // RING + 1)
                                 if kind_at(kind, k, 3) else 0)
                            nc.scalar.copy(mrows[(k - 1) % 2][:, :], misc_rows).then_inc(mrow_sb, 1)
                        which = kind_at(kind, k, 2)
                        j = step_at(kind, which, i)
                        if j is not None:
                            x0 = PIECES.before(kind, r) + piece_no(kind, k, j)
                            scale = (SCALE_A, SCALE_B)[which == "B"]
                            buf = exps[which][j % N_PROBS[which]]
                            need(act, pv_done, added(kind, r, k - 3) + j - N_PROBS[which] + 1)
                            for n, (lo, hi) in enumerate(pieces(which, j)):
                                bank = (piece_no(kind, k, j) + n) % 2
                                act.wait_ge(s2_ready, x0 + n + 1)
                                nc.scalar.activation(buf[:, lo:hi], s2[bank][:, 0:hi - lo], ACT.Exp,
                                                     scale=scale).then_inc(exp_done, 1)
                        if i == 0 and kind_at(kind, k, 3):
                            act.wait_ge(pv_done, added(kind, r, k - 3))
                            need(act, ctx_out[(k - 3) % 2], 16 * ((UP // 2) * ph + (k - 3) // 2))
                            nc.scalar.copy(csb[(k - 3) % 2][:, :], cps[:, 0:GQ]).then_inc(ctx_sb, 1)
                        if kind == "A0" and 2 <= k < 2 + 2 * NCH and i == 1:
                            high_part(2 * NCH + k - 2)
                        if kind == "A0" and 2 <= k < 2 + 2 * NCH and i == 3:
                            middle_part(2 * NCH + k - 2)
                        done = (k, i - 1) if i else (k - 1, TURNS[kind] - 1)
                        if done in EXTRA[kind]:
                            extra(kind, r, c, b, ph, *EXTRA[kind][done])

            def extra(kind, r, c, b, ph, what, w):
                preps = PREPS.before(kind, r)
                steps = PREP_STEPS.before(kind, r) + (prep_no(kind, what, w) if kind in PREPARES else 0)
                if what == "node":
                    act.wait_ge(prep_ps, steps)
                    act.wait_ge(cur_ready, CUR_FIRST + CUR_COPIES.after(kind, r))
                    nc.scalar.activation(srcT[:, bass.ds(c * T + b * S + w * CH, CH)], misc[:, :], ACT.Identity,
                                         bias=cur_bias[:, 2:3]).then_inc(node_ready, 1)
                elif what in ("q", "k"):
                    n = 2 * (what == "k") + w
                    act.wait_ge(prep_ps, steps)
                    act.wait_ge(cur_ready, CUR_FIRST + CUR_COPIES.after(kind, r))
                    need(act, written, 4 * 3 * 16 * preps)
                    bias = cur_bias[:, (what == "k"):(what == "k") + 1]
                    nc.scalar.activation(full[n % STAGES][:, :], misc[:, :], ACT.Identity, bias=bias
                                         ).then_inc(prep_full, 1)
                elif what == "v":
                    act.wait_ge(prep_ps, steps)
                    need(act, vs_ready, UP * ph)
                    nc.scalar.copy(vtok_b[:, bass.ds(b * TB * D + w * CH, CH)], misc[:, :]).then_inc(v_ready, 1)
                elif what == "va":
                    act.wait_ge(va_ps, w + 1)
                    nc.scalar.copy(vtok_a[:, w * CH:(w + 1) * CH], misc[:, :]).then_inc(va_sb, 1)
                elif what == "fin":
                    act.wait_ge(fin_ps, w + 1)
                    nc.scalar.copy(fin[:, w * CH:(w + 1) * CH], misc[:, :]).then_inc(fin_sb, 1)

            walk(act, phase)
            for w in range(NCH):
                act.wait_ge(fin_ps, NCH + w + 1)
                nc.scalar.copy(fin[:, S + w * CH:S + (w + 1) * CH], (misc, s2[0])[w][:, :]).then_inc(fin_sb, 1)

        @block.vector
        def _(dve):
            ve = nc.vector
            order = [0]

            def after(ins):
                order[0] += 1
                ins.then_inc(dve_order, 1)
                dve.wait_ge(dve_order, order[0])

            def moments(src, t0, tiles):
                for t in range(t0, t0 + tiles):
                    last = ve.bn_stats(stats[:, 6 * t:6 * t + 6], src[:, t * D:(t + 1) * D])
                after(last)
                for t in range(t0, t0 + tiles):
                    last = ve.bn_aggr(mv[:, 2 * t:2 * t + 2], stats[:, 6 * t:6 * t + 6])
                after(last)

            for s in range(RING):
                for ring in (qs[s][:, :], ks[s][:, :], vs[s][:, :, :]):
                    ve.memset(ring, 0.0).then_inc(dve_const, 1)
            for n in range(NB):
                dve.wait_ge(x_in[n], 16)
                moments(xtok, n * TB, TB)
                ve.tensor_scalar_add(rstd[:, n * TB:(n + 1) * TB], mv[:, 2 * n * TB + 1:2 * (n + 1) * TB:2], EPS_A
                                     ).then_inc(ln_stats, 1)
            for t in range(TT):
                if t % TB == 0:
                    dve.wait_ge(ln_pow, t // TB + 1)
                ve.tensor_scalar(xn[:, t * D:(t + 1) * D], xtok[:, t * D:(t + 1) * D], mv[:, 2 * t:2 * t + 1],
                                 rstd[:, t:t + 1], ALU.subtract, ALU.mult).then_inc(xn_ready, 1)

            def turn(m, bank):
                n, h = m // 2, m % 2
                w, op = n // 2 % NCH, n % 2
                dve.wait_ge(rot_ps, m + 1)
                need(dve, rope_full, n)
                ve.scalar_tensor_tensor(rope[h][:, :], bank[:, :], bias_a[:, 2 * op + h:2 * op + h + 1],
                                        table[:, h * S + w * CH:h * S + (w + 1) * CH], ALU.add, ALU.mult
                                        ).then_inc(rot_done, 1)
                if h:
                    dve.wait_ge(rot_done, m + 1)
                    need(dve, a_low, n - STAGES + 1)
                    ve.tensor_tensor(full[n % STAGES][:, :], rope[0][:, :], rope[1][:, :], ALU.add
                                     ).then_inc(rope_full, 1)

            dve.wait_ge(wa_in, 16 * 6)
            for n in range(2 * NCH):
                for h in range(2):
                    turn(2 * n + h, (s2[0], s2[1], cps, misc)[(2 * n + h) % 4])
            n = 2 * NCH - 1
            dve.wait_ge(rope_hi, n + 1)
            ve.tensor_tensor(full[n % STAGES][:, :], full[n % STAGES][:, :], parts[n % STAGES][:, 0, :],
                             ALU.subtract).then_inc(rope_res, 1)

            dve.wait_ge(wb_in, 16 * 11)
            for n in range(NODES):
                ve.tensor_scalar(comp[:, (5 * n + 3) * D:(5 * n + 4) * D], w4_sb[:, (3 * NODES + n) * D:(3 * NODES + n + 1) * D],
                                 actb[:, n:n + 1], None, ALU.mult)
                last = ve.tensor_scalar(comp[:, (5 * n + 4) * D:(5 * n + 5) * D], we_q_sb[:, n * D:(n + 1) * D],
                                        ewb[:, 3 * n:3 * n + 1], None, ALU.mult)
            last.then_inc(wo_ready, 1)

            def biases(w):
                dve.wait_ge(bias_ps, w + 1)
                if w == 0:
                    ve.tensor_tensor(vbias[:, :], misc[:, 0:3 * NODES], ewb[:, :], ALU.mult).then_inc(bias_used, 1)
                    dve.wait_ge(bias_used, 1)
                    after(ve.tensor_copy(bias_b[:, :], vbias[:, :]))
                    after(ve.tensor_tensor(bias_b[:, 2:3 * NODES:3], be_sb[:, 0:3 * NODES:3], ewb[:, 0:3 * NODES:3],
                                           ALU.mult))
                elif w == 1:
                    ve.tensor_tensor(bias_b[:, 2:3 * NODES:3], misc[:, 0:NODES], bias_b[:, 2:3 * NODES:3],
                                     ALU.add).then_inc(bias_used, 1)
                elif w == 2:
                    ve.tensor_tensor(row_o[:, :], misc[0:1, 0:128], row_o[:, :], ALU.add)
                    ve.tensor_copy(row_n[:, :], misc[0:1, 128:256]).then_inc(bias_used, 1)
                else:
                    ve.tensor_tensor(lnb[:, :], misc[:, 0:128], lnb[:, :], ALU.add).then_inc(bias_used, 1)

            biases(0)

            def last_moments(n):
                t0, tiles = FINISH[n]
                dve.wait_ge(fin_sb, (t0 + tiles) // 4)
                moments(fin, t0, tiles)
                ve.tensor_scalar_add(rstd[:, t0:t0 + tiles], mv[:, 2 * t0 + 1:2 * (t0 + tiles):2], EPS_B
                                     ).then_inc(fin_stats, 1)

            def finish(n):
                t0, tiles = FINISH[n]
                dve.wait_ge(fin_pow, n + 1)
                for t in range(t0, t0 + tiles):
                    last = ve.tensor_scalar(fin[:, t * D:(t + 1) * D], fin[:, t * D:(t + 1) * D], mv[:, 2 * t:2 * t + 1],
                                            rstd[:, t:t + 1], ALU.subtract, ALU.mult)
                after(last)
                cols = slice(t0 * D, (t0 + tiles) * D)
                f3 = fin[:, cols].rearrange("p (t d) -> p t d", d=D)
                after(ve.tensor_tensor(f3, f3, lng[:, :].unsqueeze(1).broadcast_to([128, tiles, D]), ALU.mult))
                ve.tensor_tensor(fin[:, cols], fin[:, cols], xtok[:, cols], ALU.add).then_inc(out_ready, 1)

            def phase(kind, r, c, b):
                ph = PHASES.before(kind, r)
                if kind == "T":
                    last_moments(0)
                    finish(0)
                for k in range(STEPS[kind]):
                    u = UP * ph + k
                    for i in range(TURNS[kind]):
                        if kind != "T":
                            if i == 0:
                                need(dve, max_parts, 4 * (u - 1))
                            n = steps_before(kind, k, 0) + i
                            dve.wait_ge(s1_ready, MAXIMA.before(kind, r) + n + 1)
                            for t, lo, hi in query_tiles(kind[0], i):
                                last = ve.tensor_reduce(neg_max[k % 2][:, t:t + 1], s1[n % 2][:, lo:hi], AX.X,
                                                        ALU.max, negate=True)
                            last.then_inc(max_done, 1)
                        if NORMS.per[kind] and (k, i) == ((2, 7) if kind == "T" else (SPREAD_AT[kind], 1)):
                            dve.wait_ge(sums_in, 16 * NORMS.after(kind, r))
                            cols = (HA if kind == "B0" else HB) * S // 128
                            for n in range(NORMS.per[kind]):
                                ve.reciprocal(sums[:, n * cols:(n + 1) * cols], sums[:, n * cols:(n + 1) * cols]
                                              ).then_inc(rec_ready, 1)
                        what, g = EXTRA[kind].get((k, i), ("", 0))
                        if what == "bias":
                            biases(g)
                        if what == "rot":
                            turn(g, misc)
                        if what == "xa":
                            dve.wait_ge(x_ready, 1)
                            dve.wait_ge(xa_ps, g + 1)
                            ve.tensor_tensor(xtok[:, g * CH:(g + 1) * CH], misc[:, :], xtok[:, g * CH:(g + 1) * CH],
                                             ALU.add).then_inc(xa_done, 1)

            walk(dve, phase)
            for w in range(NCH):
                dve.wait_ge(rec_in, 16 * NORMS.after("T", 0))
                dve.wait_ge(ctx_in, 16 * (S // GQ) * NORMS.after("T", 0))
                cols = slice(w * CH, (w + 1) * CH)
                ve.tensor_tensor(ctx_b[:, cols], ctx_b[:, cols], rec_b[:, cols], ALU.mult).then_inc(last_ctx, 1)
            for n in range(1, len(FINISH)):
                last_moments(n)
            for n in range(1, len(FINISH)):
                finish(n)

        @block.tensor
        def _(pe):
            te = nc.tensor

            def mm(dst, lhsT, rhs, start=True, stop=True):
                return te.matmul(dst, lhsT, rhs, start=start, stop=stop)

            pe.wait_ge(pool_const, 4)

            def transposes(batch):
                for t in range(batch * TB, (batch + 1) * TB):
                    pe.wait_ge(xn_ready, t + 1)
                    last = te.transpose(half[t // 4][:, t % 4 * 128:(t % 4 + 1) * 128], xn[:, t * D:(t + 1) * D],
                                        ident[:, :])
                    if t % 4 == 3:
                        last.then_inc(xt_ps, 1)

            def rotate(m, bank):
                chunk, w = m // 4, m % 4
                mm(bank[:, :], w_a[:, w * D:(w + 1) * D], srcT[:, chunk * CH:(chunk + 1) * CH]).then_inc(rot_ps, 1)

            def values_a(g, bank):
                for t in range(4):
                    last = mm(bank[:, t * D:(t + 1) * D], srcT[:, (4 * g + t) * D:(4 * g + t + 1) * D],
                              w_a[:, 4 * D:5 * D])
                last.then_inc(va_ps, 1)

            def products(n):
                need(pe, va_sb, min(n - 1, 2))
                need(pe, comp_sb, 3 * (n - 3))
                for w in range(3):
                    last = mm(half[n % 4][:, w * D:(w + 1) * D], we_t_sb[:, (3 * n + w) * D:(3 * n + w + 1) * D],
                              w4_sb[:, (w * NODES + n) * D:(w * NODES + n + 1) * D])
                last.then_inc(comp_ps, 1)

            transposes(0)
            pe.wait_ge(wqk_in, 16)
            for m in range(4 * NCH):
                pe.wait_ge(xt_sb, m // 4 + 1)
                need(pe, rot_done, m - 3)
                rotate(m, (s2[0], s2[1], cps, misc)[m % 4])
                if m == 3:
                    transposes(1)
                if m == 5:
                    pe.wait_ge(wb_in, 16 * 11)
                    products(0)
                if m == 7:
                    products(1)
            pe.wait_ge(wa_in, 16 * 6)
            for g in range(TB // 4):
                pe.wait_ge(xt_sb, 3 + g)
                values_a(g, half[2 + g])

            def biases(w):
                if w == 0:
                    for n in range(NODES):
                        for x in range(3):
                            last = mm(misc[:, 3 * n + x:3 * n + x + 1],
                                      w4_sb[:, (x * NODES + n) * D:(x * NODES + n + 1) * D],
                                      be_sb[:, 3 * n + x:3 * n + x + 1])
                elif w == 1:
                    pe.wait_ge(bias_used, 1)
                    pe.wait_ge(wo_ready, 1)
                    for n in range(NODES):
                        last = mm(misc[:, n:n + 1], comp[:, (5 * n + 3) * D:(5 * n + 4) * D],
                                  vbias[:, 3 * n + 2:3 * n + 3])
                elif w == 2:
                    mm(misc[0:1, 0:128], bias_a[:, 4:5], w_a[:, 5 * D:6 * D])
                    last = mm(misc[0:1, 128:256], bias_b[:, 3 * NODES - 1:3 * NODES], ident[:, :])
                else:
                    last = mm(misc[:, 0:128], ones_row[:, :], row_o[:, :])
                last.then_inc(bias_ps, 1)

            pe.wait_ge(rot_done, 4 * NCH)
            biases(0)
            for n in range(2, NODES):
                products(n)
            pe.wait_ge(comp_sb, 3 * NODES)
            pe.wait_ge(pool_const, N_CONST)

            def context(which, u, i, k, exp_no):
                pe.wait_ge(exp_done, exp_no)
                if i == 0:
                    need(pe, ctx_sb, u)
                    pe.wait_ge(vs_ready, u + 1)
                for j, at, q0 in key_tiles(which, i):
                    for g in range(q0 // GQ, S // GQ):
                        lo, hi = max(g * GQ, q0), (g + 1) * GQ
                        last = te.matmul(cps[g * VW:(g + 1) * VW, lo - g * GQ:GQ], vs[k % RING][:, j, :],
                                         exps[which][i % N_PROBS[which]][:, at + lo - q0:at + hi - q0],
                                         start=(i == 0), stop=(j == last_tile(which, g)),
                                         tile_position=(0, g * VW))
                last.then_inc(pv_done, 1)

            def release(kind, r, what, w):
                preps = PREPS.before(kind, r)
                if what == "mt":
                    return mrow_sb, UP * PHASES.before(kind, r) + w
                if what == "node":
                    return node_ready, 2 * NODE_PHASES.before(kind, r) + w + 1
                if what in ("q", "k"):
                    return prep_full, 4 * preps + 2 * (what == "k") + w + 1
                if what == "v":
                    return v_ready, NCH * preps + w + 1
                if what in ("bias", "rot", "va"):
                    return {"bias": bias_used, "rot": rot_done, "va": va_sb}[what], w + 1
                return (xa_done, w + 1) if what == "xa" else (fin_sb, w + 1)

            def bank_free(kind, r, k, i, extra):
                uses = [(u, MT_SLOT[which_turns(kind)], 0, "mt", u) for u in range(STEPS[kind]) if kind_at(kind, u, 1)]
                uses = sorted(uses + [(*at, 1, *v) for at, v in EXTRA[kind].items()])
                n = [x[:3] for x in uses].index((k, i, int(extra)))
                if n:
                    need(pe, *release(kind, r, *uses[n - 1][3:]))
                else:
                    need(pe, mrow_sb, UP * PHASES.before(kind, r) - 1)

            def extra(kind, r, c, b, what, w):
                cols = slice(w * CH, (w + 1) * CH)
                if what == "node":
                    pe.wait_ge(ctx_ready, NORMS.after(kind, r))
                    pe.wait_ge(cur_ready, CUR_FIRST + CUR_COPIES.after(kind, r))
                    mm(misc[:, :], cur[:, 2 * D:3 * D], ctx_b[:, cols], stop=False)
                    mm(misc[:, :], cur[:, 3 * D:4 * D], srcT[:, bass.ds((c - 1) * T + b * S + w * CH, CH)],
                       start=False).then_inc(prep_ps, 1)
                elif what in ("q", "k"):
                    op = int(what == "k")
                    need(pe, node_ready, 2 * NODE_PHASES.before(kind, r) + (1 if (what, w) == ("q", 0) else 2)
                         if NODE_PHASES.per[kind] else 0)
                    pe.wait_ge(cur_ready, CUR_FIRST + CUR_COPIES.after(kind, r))
                    at = (c // PREV if op else c) * T + b * S + w * CH
                    mm(misc[:, :], cur[:, op * D:(op + 1) * D], srcT[:, bass.ds(at, CH)]).then_inc(prep_ps, 1)
                elif what == "v":
                    pe.wait_ge(vsrc_in, 16 * PREPS.after(kind, r))
                    for t in range(4):
                        last = mm(misc[:, t * D:(t + 1) * D], vsrc[:, w * CH + t * 128:w * CH + (t + 1) * 128],
                                  comp[:, bass.ds(c * 5 * D + 2 * D, D)])
                    last.then_inc(prep_ps, 1)
                elif what == "bias":
                    biases(w)
                elif what == "rot":
                    pe.wait_ge(xt_sb, w // 4 + 1)
                    rotate(w, misc)
                elif what == "va":
                    values_a(w, misc)
                elif what == "xa":
                    pe.wait_ge(ctx_ready, NB)
                    for t in range(4):
                        last = mm(misc[:, t * D:(t + 1) * D], ctx_a[:, (4 * w + t) * 128:(4 * w + t + 1) * 128],
                                  w_a[:, 5 * D:6 * D])
                    last.then_inc(xa_ps, 1)
                else:
                    pe.wait_ge(ctx_ready, NORMS.after(kind, r))
                    last_node(0, w, misc, ("skip", "context"))

            def last_node(batch, w, bank, terms):
                at = (5 * (NODES - 1)) * D
                for t in range(4 * w, 4 * w + 4):
                    dst, tok = bank[:, t % 4 * D:(t % 4 + 1) * D], slice(t * 128, (t + 1) * 128)
                    src = (NODES - 1) * T + batch * S + t * 128
                    if "skip" in terms:
                        mm(dst, srcT[:, src:src + 128], comp[:, at + 4 * D:at + 5 * D],
                           start="context" in terms or t % 4 == 0, stop=False)
                        mm(dst, ones_row[:, :], row_n[:, :], start=False, stop=False)
                    if "context" in terms:
                        last = mm(dst, ctx_b[:, tok], comp[:, at + 3 * D:at + 4 * D], start=False,
                                  stop="skip" in terms or t % 4 == 3)
                if "context" in terms:
                    last.then_inc(fin_ps, 1)

            def phase(kind, r, c, b):
                ph = PHASES.before(kind, r)
                for k in range(STEPS[kind]):
                    u = UP * ph + k
                    which = kind_at(kind, k, 2)
                    for i in range(TURNS[kind]):
                        j = step_at(kind, which, i)
                        if j is not None:
                            q, ky = qs[(k - 2) % RING], ks[(k - 2) % RING]
                            if i == 0:
                                pe.wait_ge(mrow_in[(k - 2) % RING], 16 * (2 * ph + (k - 2) // RING + 1))
                            for n, (lo, hi) in enumerate(pieces(which, j)):
                                x0 = piece_no(kind, k, j) + n
                                bank = s2[x0 % 2]
                                need(pe, exp_done, PIECES.before(kind, r) + x0 - 1)
                                for t, at, q0 in key_tiles(which, j):
                                    first, end = max(lo, at), min(hi, at + S - q0)
                                    if first >= end:
                                        continue
                                    diagonal = which == "A" and first == at
                                    last = mm(bank[:, first - lo:end - lo], ky[0:KALL, t * 128:(t + 1) * 128],
                                              q[0:KALL, q0 + first - at:q0 + end - at], stop=not diagonal)
                                    if diagonal:
                                        last = mm(bank[:, at - lo:at - lo + 128], ident_h[:, :], mask_k[:, :],
                                                  start=False)
                                last.then_inc(s2_ready, 1)
                        if kind != "T":
                            q, ky = qs[k % RING], ks[k % RING]
                            if i == 0:
                                pe.wait_ge(qk_in[k % RING], 32 * (2 * ph + k // RING + 1))
                            n = steps_before(kind, k, 0) + i
                            need(pe, max_done, MAXIMA.before(kind, r) + n - 1)
                            for t, at, end in query_tiles(kind[0], i):
                                for lo, hi in pieces(kind[0], i):
                                    lo, hi = max(lo, at), min(hi, end)
                                    if lo >= hi:
                                        continue
                                    diagonal = kind[0] == "A" and hi == end
                                    last = mm(s1[n % 2][:, lo:hi], q[0:KROW, t * 128:(t + 1) * 128],
                                              ky[0:KROW, lo - at:hi - at], stop=not diagonal)
                                    if diagonal:
                                        last = mm(s1[n % 2][:, end - 128:end], ident_h[:, :], mask_q[:, :],
                                                  start=False)
                            last.then_inc(s1_ready, 1)
                        if i == 0 and kind_at(kind, k, 3):
                            context(kind_at(kind, k, 3), u - 3, N_TILES[kind_at(kind, k, 3)] - 1, k - 3,
                                    PIECES.before(kind, r) + pieces_before(kind, k))
                        elif j:
                            context(which, u - 2, j - 1, k - 2, PIECES.before(kind, r) + piece_no(kind, k, j))
                        if i == MT_SLOT[which_turns(kind)] and kind_at(kind, k, 1):
                            pe.wait_ge(max_parts, 4 * u)
                            bank_free(kind, r, k, i, False)
                            te.transpose(misc_rows, mparts[(k - 1) % 2][:, :], ident_h[:, :]).then_inc(mt_ready, 1)
                        if (k, i) in EXTRA[kind]:
                            bank_free(kind, r, k, i, True)
                            extra(kind, r, c, b, *EXTRA[kind][k, i])

            walk(pe, phase)
            pe.wait_ge(fin_sb, NCH)
            for w in range(NCH):
                last_node(1, w, (misc, s2[0])[w], ("skip",))
            for w in range(NCH):
                pe.wait_ge(last_ctx, w + 1)
                last_node(1, w, (misc, s2[0])[w], ("context",))


def rotation_tables():
    import numpy as np

    half = DA // 2
    inv = (1.0 / np.float32(10000.0) ** (np.arange(half, dtype=np.float32) / np.float32(half))).astype(np.float32)
    angles = np.outer(np.arange(S, dtype=np.float32), inv).astype(np.float32)
    cos, sin = np.cos(angles).T, np.sin(angles).T
    cos = np.tile(np.concatenate([cos, cos]), (HA, 1))
    sin = np.tile(np.concatenate([-sin, sin]), (HA, 1))
    return np.ascontiguousarray(cos, dtype=np.float32), np.ascontiguousarray(sin, dtype=np.float32)


def kernel(**inputs):
    import numpy as np
    import concourse.bacc as bacc
    from concourse.bass_utils import run_bass_kernel_spmd as run

    a = {k.replace("L0_", ""): np.asarray(v) for k, v in inputs.items()}
    swap = np.arange(D).reshape(HA, 2, DA // 2)[:, ::-1].reshape(-1)
    w, bias = a["attn_qkv_w"], a["attn_qkv_b"]
    wq_a, wk_a, wv_a = w[0:D], w[D:2 * D], w[2 * D:3 * D]
    bq_a, bk_a, bv_a = bias[0:D], bias[D:2 * D], bias[2 * D:3 * D]
    order = np.array([e for node, _ in edges() for e in node])
    cos, sin = rotation_tables()
    arrays = {
        "x": a["attn_x"].reshape(T, D),
        "w_qk": np.concatenate([wq_a.T, wq_a[swap].T, wk_a.T, wk_a[swap].T], axis=1),
        "w_va": wv_a.T, "w_oa": a["attn_out_w"].T,
        "b_a": np.stack([bq_a, bq_a[swap], bk_a, bk_a[swap], bv_a], axis=1),
        "out_b": a["attn_out_b"].reshape(1, D),
        "cos": cos, "sin": sin,
        "ew": a["ffn_ew"].reshape(1, -1), "act_w": a["ffn_act_w"].reshape(1, -1),
        "we_t": a["ffn_We"][order].transpose(2, 0, 1).reshape(D, -1),
        "we_q": a["ffn_We"][order[0::3]],
        "be": a["ffn_be"][order].T,
        "wq": a["ffn_Wq"], "wk": a["ffn_Wk"], "wv": a["ffn_Wv"], "wo": a["ffn_Wo"],
        "ln_g": a["ffn_ln_g"].reshape(1, D), "ln_b": a["ffn_ln_b"].reshape(1, D),
    }
    arrays = {k: np.ascontiguousarray(v) for k, v in arrays.items()}
    nc = bacc.Bacc("TRN2", target_bir_lowering=False, num_devices=1)
    args = [nc.dram_tensor(f"in_{k}", v.shape, mybir.dt.from_np(v.dtype), kind="ExternalInput").ap()
            for k, v in arrays.items()]
    out = nc.dram_tensor("out", (T, D), F32, kind="ExternalOutput").ap()
    dual_attention_kernel(nc, *args, out)
    r = run(nc, [{f"in_{k}": v for k, v in arrays.items()}], core_ids=[0])
    return r.results[0]["out"].reshape(NB, S, D)
```
